# Optimizing a Trainium2 kernel written in Bass

```python
import numpy as np
import jax
import jax.numpy as jnp

def _softmax(x, axis=-1):
    return jax.nn.softmax(x, axis=axis)

def _gelu(x):
    return jax.nn.gelu(x, approximate=True)

def _silu(x):
    return jax.nn.silu(x)

def _sigmoid(x):
    return jax.nn.sigmoid(x)

def _layernorm(x, axis=-1, eps=1e-05):
    m = jnp.mean(x, axis=axis, keepdims=True)
    v = jnp.var(x, axis=axis, keepdims=True)
    return (x - m) / jnp.sqrt(v + eps)

def _scatter_add(tgt, idx, src, axis=0):
    return tgt.at[idx].add(src)

def _segment_sum(src, seg, n):
    return jax.ops.segment_sum(src, seg, n)
kernel_name = 'mk_sandwich_d1_jaxref_r8_bc9dca'

def setup_inputs(seed: int=0):
    np.random.seed(seed)
    _w = jnp.asarray

    def _L0_attn_setup():
        import jax, jax.numpy as jnp
        import numpy as np
        B, S, C, H = (2, 512, 128, 8)
        D = C // H
        KCONV = 7

        def _ripple(x, Wqkv, Wo, conv_w):
            b, s, c = x.shape
            d = c // H
            qkv = x @ Wqkv
            q, k, v = jnp.split(qkv, 3, axis=-1)

            def heads(t):
                return t.reshape(b, s, H, d).transpose(0, 2, 1, 3)
            qh, kh, vh = (heads(q), heads(k), heads(v))
            n_pow = int(np.floor(np.log2(s))) + 1
            offsets = jnp.concatenate([jnp.zeros((1,), jnp.int32), (2 ** jnp.arange(n_pow)).astype(jnp.int32)])
            pos = jnp.arange(s, dtype=jnp.int32)[:, None] - offsets[None, :]
            valid = pos >= 0
            posc = jnp.clip(pos, 0)
            kg = kh[:, :, posc]
            vg = vh[:, :, posc]
            sc = jnp.einsum('bhsd,bhskd->bhsk', qh, kg) / np.sqrt(d)
            sc = jnp.where(valid[None, None], sc, -jnp.inf)
            w = jax.nn.softmax(sc, axis=-1)
            tele = jnp.einsum('bhsk,bhskd->bhsd', w, vg)
            vpad = jnp.pad(v, ((0, 0), (KCONV - 1, 0), (0, 0)))
            conv = jax.lax.conv_general_dilated(vpad.transpose(0, 2, 1), conv_w[:, None, :], window_strides=(1,), padding='VALID', feature_group_count=c, dimension_numbers=('NCH', 'OIH', 'NCH')).transpose(0, 2, 1)
            conv_h = conv.reshape(b, s, H, d).transpose(0, 2, 1, 3)
            fq = jax.nn.elu(qh) + 1.0
            fk = jax.nn.elu(kh) + 1.0
            kv = jnp.einsum('bhsd,bhse->bhde', fk, vh)
            z = jnp.einsum('bhsd,bhd->bhs', fq, fk.sum(2))
            low = jnp.einsum('bhsd,bhde->bhse', fq, kv) / (z[..., None] + 1e-06)
            h = (tele + conv_h + low).transpose(0, 2, 1, 3).reshape(b, s, c)
            return h @ Wo
        key = jax.random.key(seed)
        k1, k2, k3, k4 = jax.random.split(key, 4)
        x = jax.random.normal(k1, (B, S, C), jnp.float32)
        Wqkv = jax.random.normal(k2, (C, 3 * C), jnp.float32) * (1.0 / np.sqrt(C))
        Wo = jax.random.normal(k3, (C, C), jnp.float32) * (1.0 / np.sqrt(C))
        conv_w = jax.random.normal(k4, (C, KCONV), jnp.float32) * (1.0 / np.sqrt(KCONV))
        return {'x': x, 'Wqkv': Wqkv, 'Wo': Wo, 'conv_w': conv_w}
    _L0_attn_in = _L0_attn_setup()

    def _L0_ffn_setup():
        import jax, jax.numpy as jnp
        import numpy as np
        B, S, D, E, H, K = (4, 256, 128, 8, 64, 2)
        key = jax.random.key(seed)
        ks = jax.random.split(key, 11)
        sc = 0.02
        return {'x': jax.random.normal(ks[0], (B, S, D), dtype=jnp.float32), 'gate_W': jax.random.normal(ks[1], (D, E), dtype=jnp.float32) * sc, 'W1': jax.random.normal(ks[2], (E, D, H), dtype=jnp.float32) * sc, 'b1': jnp.zeros((E, H), dtype=jnp.float32), 'W2': jax.random.normal(ks[3], (E, H, D), dtype=jnp.float32) * sc, 'b2': jnp.zeros((E, D), dtype=jnp.float32), 'Ws1': jax.random.normal(ks[4], (D, H), dtype=jnp.float32) * sc, 'bs1': jnp.zeros((H,), dtype=jnp.float32), 'Ws2': jax.random.normal(ks[5], (H, D), dtype=jnp.float32) * sc, 'bs2': jnp.zeros((D,), dtype=jnp.float32), 'route_scale': jnp.ones((), dtype=jnp.float32)}
    _L0_ffn_in = _L0_ffn_setup()
    _d = {'L0_attn_x': _L0_attn_in['x'], 'L0_attn_Wqkv': _L0_attn_in['Wqkv'], 'L0_attn_Wo': _L0_attn_in['Wo'], 'L0_attn_conv_w': _L0_attn_in['conv_w'], 'L0_ffn_gate_W': _L0_ffn_in['gate_W'], 'L0_ffn_W1': _L0_ffn_in['W1'], 'L0_ffn_b1': _L0_ffn_in['b1'], 'L0_ffn_W2': _L0_ffn_in['W2'], 'L0_ffn_b2': _L0_ffn_in['b2'], 'L0_ffn_Ws1': _L0_ffn_in['Ws1'], 'L0_ffn_bs1': _L0_ffn_in['bs1'], 'L0_ffn_Ws2': _L0_ffn_in['Ws2'], 'L0_ffn_bs2': _L0_ffn_in['bs2'], 'L0_ffn_route_scale': _L0_ffn_in['route_scale']}
    _x0 = _d['L0_attn_x']
    _d['L0_attn_x'] = jax.random.normal(jax.random.fold_in(jax.random.key(seed), 1), (4, 1024, 128), dtype=_x0.dtype)
    del _x0
    return _d

def reference(L0_attn_x, L0_attn_Wqkv, L0_attn_Wo, L0_attn_conv_w, L0_ffn_gate_W, L0_ffn_W1, L0_ffn_b1, L0_ffn_W2, L0_ffn_b2, L0_ffn_Ws1, L0_ffn_bs1, L0_ffn_Ws2, L0_ffn_bs2, L0_ffn_route_scale):

    def _L0_attn_ref(x, Wqkv, Wo, conv_w):
        import jax, jax.numpy as jnp
        import numpy as np
        B, S, C, H = (2, 512, 128, 8)
        D = C // H
        KCONV = 7

        def _ripple(x, Wqkv, Wo, conv_w):
            b, s, c = x.shape
            d = c // H
            qkv = x @ Wqkv
            q, k, v = jnp.split(qkv, 3, axis=-1)

            def heads(t):
                return t.reshape(b, s, H, d).transpose(0, 2, 1, 3)
            qh, kh, vh = (heads(q), heads(k), heads(v))
            n_pow = int(np.floor(np.log2(s))) + 1
            offsets = jnp.concatenate([jnp.zeros((1,), jnp.int32), (2 ** jnp.arange(n_pow)).astype(jnp.int32)])
            pos = jnp.arange(s, dtype=jnp.int32)[:, None] - offsets[None, :]
            valid = pos >= 0
            posc = jnp.clip(pos, 0)
            kg = kh[:, :, posc]
            vg = vh[:, :, posc]
            sc = jnp.einsum('bhsd,bhskd->bhsk', qh, kg) / np.sqrt(d)
            sc = jnp.where(valid[None, None], sc, -jnp.inf)
            w = jax.nn.softmax(sc, axis=-1)
            tele = jnp.einsum('bhsk,bhskd->bhsd', w, vg)
            vpad = jnp.pad(v, ((0, 0), (KCONV - 1, 0), (0, 0)))
            conv = jax.lax.conv_general_dilated(vpad.transpose(0, 2, 1), conv_w[:, None, :], window_strides=(1,), padding='VALID', feature_group_count=c, dimension_numbers=('NCH', 'OIH', 'NCH')).transpose(0, 2, 1)
            conv_h = conv.reshape(b, s, H, d).transpose(0, 2, 1, 3)
            fq = jax.nn.elu(qh) + 1.0
            fk = jax.nn.elu(kh) + 1.0
            kv = jnp.einsum('bhsd,bhse->bhde', fk, vh)
            z = jnp.einsum('bhsd,bhd->bhs', fq, fk.sum(2))
            low = jnp.einsum('bhsd,bhde->bhse', fq, kv) / (z[..., None] + 1e-06)
            h = (tele + conv_h + low).transpose(0, 2, 1, 3).reshape(b, s, c)
            return h @ Wo
        return x + _ripple(x, Wqkv, Wo, conv_w)

    def _L0_ffn_ref(x, gate_W, W1, b1, W2, b2, Ws1, bs1, Ws2, bs2, route_scale):
        import jax, jax.numpy as jnp
        import numpy as np
        B, S, D, E, H, K = (4, 256, 128, 8, 64, 2)
        scores = jax.nn.sigmoid(x @ gate_W) * route_scale
        topk_scores, topk_idx = jax.lax.top_k(scores, K)
        topk_w = topk_scores / topk_scores.sum(-1, keepdims=True)
        onehot = jax.nn.one_hot(topk_idx, E, dtype=x.dtype)
        gate_full = jnp.einsum('bsk,bske->bse', topk_w, onehot)
        h = jax.nn.gelu(jnp.einsum('bsd,edh->bseh', x, W1) + b1, approximate=False)
        y = jnp.einsum('bseh,ehd->bsed', h, W2) + b2
        expert_out = jnp.einsum('bse,bsed->bsd', gate_full, y)
        shared = jax.nn.gelu(x @ Ws1 + bs1, approximate=False) @ Ws2 + bs2
        return expert_out + shared
    x = L0_attn_x
    x = x + _layernorm(_L0_attn_ref(_layernorm(x, axis=-1), L0_attn_Wqkv, L0_attn_Wo, L0_attn_conv_w), axis=-1)
    x = x + _layernorm(_L0_ffn_ref(_layernorm(x, axis=-1), L0_ffn_gate_W, L0_ffn_W1, L0_ffn_b1, L0_ffn_W2, L0_ffn_b2, L0_ffn_Ws1, L0_ffn_bs1, L0_ffn_Ws2, L0_ffn_bs2, L0_ffn_route_scale), axis=-1)
    return x

_drawn_inputs = setup_inputs


def setup_inputs(seed=0):
    import zlib

    import numpy as np

    out = dict(_drawn_inputs(seed))
    spreads = {'L0_ffn_b1': (0.0, 0.321),
     'L0_ffn_b2': (0.0, 0.1),
     'L0_ffn_bs1': (0.0, 0.1),
     'L0_ffn_bs2': (0.0, 0.1)}
    factors = {}
    for name, (base, spread) in spreads.items():
        noise = np.random.default_rng([zlib.crc32(name.encode()), seed]).standard_normal(out[name].shape)
        drawn = base * np.exp(spread * noise) if base else spread * noise
        out[name] = jnp.asarray(drawn.astype(out[name].dtype))
    for name, factor in factors.items():
        out[name] = (out[name] * factor).astype(out[name].dtype)
    return out
```

```python
from contextlib import ExitStack

import numpy as np

import concourse.bass as bass
from concourse import mybir

F32 = mybir.dt.float32
BF16 = mybir.dt.bfloat16
ALU = mybir.AluOpType
ACT = mybir.ActivationFunctionType
AX_X = mybir.AxisListType.X

P = 128
HEADS = 8
HD = P // HEADS
TAPS = 7
EXPERTS = 8
HID = 64
T = 1024
NT = T // P
HALF = 512
TPH = HALF // P
EPS = 1e-5
BIG = 3.0e38
PRE = 512
VPRE = 64

LOW = -1
TERMS = [1, 2, 4, 8, 16, LOW, 32, 64, 512, 256, 0, 128]
NM = len(TERMS)
M_LOW = TERMS.index(LOW)
M_TILES = TERMS.index(512)
M_128 = TERMS.index(128)
SLOTS, QUADS = 3, 4
CH = 5

N_DMA = 16
N_PSA_FULL, N_PSA_FREE = 16, 14
N_PRODUCTS = 11
N_PSF_FULL, N_PSF_FREE = 24, 14
N_GATE_STEPS = 24
N_SOFTMAX_STEPS = 5
N_CONV_STEPS = 2 * TAPS - 1


def upto(b, per_batch, n):
    return b * per_batch + n


class Chain:

    def __init__(self, sem, per_batch):
        self.sem, self.per_batch = sem, per_batch

    def start(self, eng, b):
        self.eng, self.b, self.n = eng, b, 0

    def __call__(self, ins):
        self.n += 1
        ins.then_inc(self.sem, 1)
        self.eng.wait_ge(self.sem, upto(self.b, self.per_batch, self.n))

    def done(self):
        assert self.n == self.per_batch, (self.n, self.per_batch)


def block_kernel(nc, x, Wqkv, Wo, conv_w, gate_W, W1, b1, W2, b2, Ws1, bs1, Ws2, bs2, route_scale, out):
    B = x.shape[0]
    x_tok = x.rearrange("b (j p) c -> b p j c", p=P)
    out_tok = out.rearrange("b (j p) c -> b p j c", p=P)

    with ExitStack() as ctx:
        def sb(name, shape, dt=F32):
            return ctx.enter_context(nc.sbuf_tensor(name, shape, dt))

        def psum(name, shape, dt=F32):
            return ctx.enter_context(nc.psum_tensor(name, shape, dt))

        def sem(name):
            return ctx.enter_context(nc.semaphore(name))

        ctx.enter_context(nc.allow_non_contiguous_dma(reason="small bias vectors"))

        ident = sb("ident", [P, P])
        identb = sb("identb", [P, P], BF16)
        head_sel = sb("head_sel", [P, HEADS])
        head_mask = sb("head_mask", [P, P])
        slot_sel = sb("slot_sel", [P, SLOTS, 32])
        ksum_sel = sb("ksum_sel", [P, 32])
        mask = sb("mask", [P, NT, NM, HEADS])
        first_pref = sb("first_pref", [P, NT, EXPERTS])
        gate_sel = sb("gate_sel", [24, 4, P], BF16)
        neg_half = sb("neg_half", [P, NT])
        wqkv = sb("wqkv", [P, 3 * P])
        wo = sb("wo", [P, P])
        cw = sb("cw", [P, TAPS])
        w1 = sb("w1", [P, CH * P])
        w2 = sb("w2", [P, CH, P])
        b1c = sb("b1c", [P, 4])
        bs1c = sb("bs1c", [P, 1])
        rscale = sb("rscale", [P, 1])
        row_mean = sb("row_mean", [P, 1 + CH])

        x_in = sb("x_in", [P, NT, P])
        x_res = sb("x_res", [P, NT, P])
        xn = sb("xn", [P, NT, P])
        xn_res = sb("xn_res", [P, NT, P])
        yc = sb("yc", [P, NT, P])
        x2 = sb("x2", [P, NT, P])
        xn3 = sb("xn3", [P, NT, P])
        fk_tok = sb("fk_tok", [P, NT, P])
        v_tok = sb("v_tok", [P, NT, P])
        bn = sb("bn", [P, NT, 6])
        mv = sb("mv", [P, NT, 2])
        neg_mean = sb("neg_mean", [P, NT])
        neg_mean3 = sb("neg_mean3", [P, NT])
        var1, rstd1, nmr1 = sb("var1", [P, NT]), sb("rstd1", [P, NT]), sb("nmr1", [P, NT])
        ss2, var2, rstd2 = sb("ss2", [P, NT]), sb("var2", [P, NT]), sb("rstd2", [P, NT])
        ss3, var3, rstd3, nmr3 = sb("ss3", [P, NT]), sb("var3", [P, NT]), sb("rstd3", [P, NT]), sb("nmr3", [P, NT])
        ss4, var4, rstd4 = sb("ss4", [P, NT]), sb("var4", [P, NT]), sb("rstd4", [P, NT])
        squares2, squares3, squares4 = (sb(f"squares{i}", [P, NT, P]) for i in (2, 3, 4))
        logit = sb("logit", [P, NT, NM, HEADS])
        top = sb("top", [P, NT, HEADS])
        prob = sb("prob", [P, NT, NM, HEADS])
        den = sb("den", [P, NT, HEADS])
        rden = sb("rden", [P, NT, HEADS])
        zden = sb("zden", [P, NT, HEADS])
        wgt = sb("wgt", [P, NT, NM, HEADS])
        terms = sb("terms", [P, 2, NM, P])

        xnT = sb("xnT", [P, T])
        kT = sb("kT", [P, PRE + T])
        vT = sb("vT", [P, VPRE + T])
        qT = sb("qT", [P, T])
        kexp, fkT = sb("kexp", [P, T]), sb("fkT", [P, T])
        qexp, fqT = sb("qexp", [P, T]), sb("fqT", [P, T])
        ksum = sb("ksum", [P, 1])
        kv = sb("kv", [P, P])
        prods = sb("prods", [P, 2 * QUADS, T])
        scoresT = sb("scoresT", [P, T])
        convT = sb("convT", [P, T])
        tapT = sb("tapT", [P, T])
        hT = sb("hT", [P, T])

        x3T = sb("x3T", [P, T])
        gate_shared = sb("gate_shared", [P, T])
        gexp = sb("gexp", [P, NT, EXPERTS])
        gtmp = [sb(f"gtmp{i}", [P, NT, EXPERTS]) for i in range(10)]
        gmax = [sb(f"gmax{i}", [P, NT]) for i in range(6)]
        gparts = sb("gparts", [P, NT, 3, EXPERTS], BF16)
        gT = sb("gT", [24, T], BF16)
        hid = sb("hid", [P, CH, T])
        y_out = sb("y_out", [P, NT, P])

        psA = psum("psA", [P, 2, HALF])
        psG = psum("psG", [P, 2, HALF])
        psH = psum("psH", [P, HALF])
        psY = psum("psY", [P, HALF])
        psF = psum("psF", [P, 2, HALF])

        wqkv_ld, conv_ld, wo_ld, ffn_ld = sem("wqkv_ld"), sem("conv_ld"), sem("wo_ld"), sem("ffn_ld")
        x_in_ld, x_res_ld, out_stored = sem("x_in_ld"), sem("x_res_ld"), sem("out_stored")
        pool_set, zeros_set, consts_ready = sem("pool_set"), sem("zeros_set"), sem("consts_ready")
        w_zeroed, w_means, w_centred = sem("w_zeroed"), sem("w_means"), sem("w_centred")
        stats1, mean_kept = sem("stats1"), sem("mean_kept")
        bn_done = sem("bn_done")
        ln1_ready, ln2_ready, ln3_ready, ln4_ready = sem("ln1_ready"), sem("ln2_ready"), sem("ln3_ready"), sem("ln4_ready")
        ln1_step, ln2_step, ln3_step, ln4_step = sem("ln1_step"), sem("ln2_step"), sem("ln3_step"), sem("ln4_step")
        xn_ready, xn_kept = sem("xn_ready"), sem("xn_kept")
        psA_full, psA_free, scores_read = sem("psA_full"), sem("psA_free"), sem("scores_read")
        k_feat, q_feat = sem("k_feat"), sem("q_feat")
        fk_ready, fq_ready = sem("fk_ready"), sem("fq_ready")
        kv_summed, kv_ready = sem("kv_summed"), sem("kv_ready")
        prod_ready, group_summed = sem("prod_ready"), sem("group_summed")
        logit_ready, prob_ready, softmax_step = sem("logit_ready"), sem("prob_ready"), sem("softmax_step")
        shift1_ready, shift2_ready, shift1_used = sem("shift1_ready"), sem("shift2_ready"), sem("shift1_used")
        terms_ready, terms_summed = sem("terms_ready"), sem("terms_summed")
        conv_step, hT_ready, y_ready, yc_ready = sem("conv_step"), sem("hT_ready"), sem("y_ready"), sem("yc_ready")
        ss2_ready, x2_ready, ss3_ready, xn3_ready = sem("ss2_ready"), sem("x2_ready"), sem("ss3_ready"), sem("xn3_ready")
        psF_full, psF_free, gated = sem("psF_full"), sem("psF_free"), sem("gated")
        gate_step = sem("gate_step")
        ss4_ready, out_ready = sem("ss4_ready"), sem("out_ready")

        softmax_chain = Chain(softmax_step, N_SOFTMAX_STEPS)
        gate_chain = Chain(gate_step, N_GATE_STEPS)
        conv_chain = Chain(conv_step, N_CONV_STEPS)

        def bank(tile):
            return tile // TPH, bass.ts(tile % TPH, P)

        block = ctx.enter_context(nc.Block())

        @block.sync
        def _(sp):
            sp.dma_start(x_in[:], x_tok[0]).then_inc(x_in_ld, 16)
            sp.dma_start(wqkv[:], Wqkv).then_inc(wqkv_ld, 16)
            sp.dma_start(x_res[:], x_tok[0]).then_inc(x_res_ld, 16)
            sp.dma_start(cw[:], conv_w).then_inc(conv_ld, 16)
            sp.dma_start(wo[:], Wo).then_inc(wo_ld, 16)
            sp.wait_ge(w_zeroed, 2)
            sp.dma_start(w1[:, 0:EXPERTS * HID].rearrange("d (e h) -> d e h", e=EXPERTS),
                         W1.rearrange("e d h -> d e h")).then_inc(ffn_ld, 16)
            sp.dma_start(w1[:, 4 * P:4 * P + EXPERTS], gate_W).then_inc(ffn_ld, 16)
            sp.dma_start(w1[:, 4 * P + HID:5 * P], Ws1).then_inc(ffn_ld, 16)
            sp.dma_start(w2[:, 0:4, :], W2.rearrange("(c e) h n -> (e h) c n", e=2)).then_inc(ffn_ld, 16)
            for part in range(3):
                sp.dma_start(w2[8 * part:8 * part + 8, 4, :], b2).then_inc(ffn_ld, 16)
            sp.dma_start(w2[24:25, 4, :], bs2.rearrange("(a n) -> a n", a=1)).then_inc(ffn_ld, 16)
            sp.dma_start(w2[HID:P, 4, :], Ws2).then_inc(ffn_ld, 16)
            sp.dma_start(b1c[:], b1.rearrange("(c e) h -> (e h) c", e=2)).then_inc(ffn_ld, 16)
            sp.dma_start(bs1c[HID:P, :], bs1.rearrange("(h a) -> h a", a=1)).then_inc(ffn_ld, 16)
            sp.dma_start(rscale[:], route_scale.rearrange("(a n) -> a n", a=1).to_broadcast([P, 1])).then_inc(ffn_ld, 16)

            def load_next(b):
                sp.wait_ge(xn_ready, upto(b, NT, NT))
                sp.dma_start(x_in[:], x_tok[b + 1]).then_inc(x_in_ld, 16)

            def load_residual(b):
                sp.wait_ge(x2_ready, upto(b, NT, 0))
                sp.dma_start(x_res[:], x_tok[b]).then_inc(x_res_ld, 16)

            def stores(b):
                sp.wait_ge(out_ready, upto(b, NT, NT))
                sp.dma_start(out_tok[b], y_out[:]).then_inc(out_stored, 16)

            load_next(0)
            for b in range(1, B):
                if b < B - 1:
                    load_next(b)
                load_residual(b)
                stores(b - 1)
            stores(B - 1)
            sp.wait_ge(out_stored, 16 * B)

        N_FFN_LD = 16 * 12

        @block.gpsimd
        def _(pool):
            nc.gpsimd.memset(ident[:], 0.0)
            nc.gpsimd.memset(head_sel[:], 1.0)
            nc.gpsimd.memset(head_mask[:], 1.0)
            nc.gpsimd.memset(slot_sel[:], 0.0)
            nc.gpsimd.memset(neg_half[:], -0.5)
            nc.gpsimd.memset(gate_sel[:], 0.0)
            nc.gpsimd.memset(mask[:], 0.0)
            for e in range(EXPERTS):
                last = nc.gpsimd.memset(first_pref[:, :, e:e + 1], float(EXPERTS - e))
            last.then_inc(pool_set, 1)
            pool.wait_ge(pool_set, 1)
            nc.gpsimd.affine_select(out=ident[:], in_=ident[:], compare_op=ALU.not_equal, fill=1.0, base=0,
                                    pattern=[[-1, P]], channel_multiplier=1).then_inc(pool_set, 1)
            nc.gpsimd.affine_select(out=head_sel[:], in_=head_sel[:], compare_op=ALU.is_ge, fill=0.0, base=0,
                                    pattern=[[-HD, HEADS]], channel_multiplier=1)
            v = head_mask[:].rearrange("p (h d) -> p h d", h=HEADS)
            nc.gpsimd.affine_select(out=v, in_=v, compare_op=ALU.is_ge, fill=0.0, base=0,
                                    pattern=[[-HD, HEADS], [0, HD]], channel_multiplier=1).then_inc(pool_set, 1)
            pool.wait_ge(pool_set, 3)
            nc.gpsimd.affine_select(out=head_sel[:], in_=head_sel[:], compare_op=ALU.is_ge, fill=0.0, base=HD - 1,
                                    pattern=[[HD, HEADS]], channel_multiplier=-1)
            nc.gpsimd.affine_select(out=v, in_=v, compare_op=ALU.is_ge, fill=0.0, base=HD - 1,
                                    pattern=[[HD, HEADS], [0, HD]], channel_multiplier=-1).then_inc(pool_set, 1)
            pool.wait_ge(pool_set, 4)
            for s in range(SLOTS):
                nc.gpsimd.tensor_copy(slot_sel[:, s, HEADS * s:HEADS * s + HEADS], head_sel[:])
            for m, off in enumerate(TERMS):
                v = mask[:, :, m, :]
                if off == LOW:
                    last = nc.gpsimd.memset(v, -BIG)
                else:
                    last = nc.gpsimd.affine_select(out=v, in_=v, compare_op=ALU.is_ge, fill=-BIG, base=-off,
                                                   pattern=[[P, NT], [0, HEADS]], channel_multiplier=1)
            for part in range(3):
                v = gate_sel[:].rearrange("r c (a n) -> r c a n", a=2)
                nc.gpsimd.affine_select(out=v, in_=v, compare_op=ALU.not_equal, fill=1.0, base=-EXPERTS * part,
                                        pattern=[[-2, 4], [-1, 2], [0, HID]],
                                        channel_multiplier=1).then_inc(pool_set, 1)
                pool.wait_ge(pool_set, 5 + part)
            nc.gpsimd.memset(kT[:, 0:PRE], 0.0)
            nc.gpsimd.memset(vT[:, 0:VPRE], 0.0).then_inc(consts_ready, 1)

            def rstd_of(var, src, scale, rstd, step, per, n, b):
                nc.gpsimd.tensor_scalar(var[:], src, scale, EPS, ALU.mult, ALU.add).then_inc(step, 1)
                pool.wait_ge(step, upto(b, per, n + 1))
                return nc.gpsimd.tensor_tensor(rstd[:], var[:], neg_half[:], ALU.pow)

            def ln1(b):
                pool.wait_ge(stats1, upto(b, 1, 1))
                nc.gpsimd.tensor_scalar(neg_mean[:], mv[:, :, 0], -1.0, 0.0, ALU.mult, ALU.add)
                rstd_of(var1, mv[:, :, 1], 1.0, rstd1, ln1_step, 2, 0, b).then_inc(ln1_step, 1)
                pool.wait_ge(ln1_step, upto(b, 2, 2))
                nc.gpsimd.tensor_tensor(nmr1[:], neg_mean[:], rstd1[:], ALU.mult).then_inc(ln1_ready, 1)

            def conv(b, first):
                pool.wait_ge(psA_free, upto(b, N_PSA_FREE, 6))
                if first:
                    pool.wait_ge(conv_ld, 16)
                else:
                    pool.wait_ge(hT_ready, upto(b, 2, 0))
                conv_chain.start(pool, b)
                conv_chain(nc.gpsimd.tensor_scalar(convT[:], vT[:, VPRE:VPRE + T], cw[:, TAPS - 1:TAPS], 0.0,
                                                   ALU.mult, ALU.add))
                for shift in range(1, TAPS):
                    conv_chain(nc.gpsimd.tensor_scalar(tapT[:], vT[:, VPRE - shift:VPRE - shift + T],
                                                       cw[:, TAPS - 1 - shift:TAPS - shift], 0.0,
                                                       ALU.mult, ALU.add))
                    conv_chain(nc.gpsimd.tensor_tensor(convT[:], convT[:], tapT[:], ALU.add))
                conv_chain.done()

            def ln2(b):
                pool.wait_ge(ss2_ready, upto(b, 1, 1))
                rstd_of(var2, ss2[:], 1.0 / P, rstd2, ln2_step, 1, 0, b).then_inc(ln2_ready, 1)

            def ln3(b):
                pool.wait_ge(ss3_ready, upto(b, 1, 1))
                rstd_of(var3, ss3[:], 1.0 / P, rstd3, ln3_step, 2, 0, b).then_inc(ln3_step, 1)
                pool.wait_ge(ln3_step, upto(b, 2, 2))
                nc.gpsimd.tensor_tensor(nmr3[:], neg_mean3[:], rstd3[:], ALU.mult).then_inc(ln3_ready, 1)

            def ln4(b):
                pool.wait_ge(ss4_ready, upto(b, 1, 1))
                rstd_of(var4, ss4[:], 1.0 / P, rstd4, ln4_step, 1, 0, b).then_inc(ln4_ready, 1)

            def keep_mean(b):
                nc.gpsimd.tensor_scalar(neg_mean3[:], neg_mean[:], 1.0, 0.0, ALU.mult, ALU.add).then_inc(mean_kept, 1)
                pool.wait_ge(mean_kept, upto(b, 1, 1))

            ln1(0)
            for b in range(B):
                if b:
                    ln3(b - 1)
                conv(b, b == 0)
                keep_mean(b)
                if b < B - 1:
                    ln1(b + 1)
                if b:
                    ln4(b - 1)
                ln2(b)
            ln3(B - 1)
            ln4(B - 1)

        @block.scalar
        def _(act):
            def copy(dst, src):
                return nc.scalar.activation(dst, src, ACT.Copy)

            def evacuate(b, use, half, dst):
                act.wait_ge(psA_full, upto(b, N_PSA_FULL, 2 * use + half + 1))
                copy(dst, psA[:, half, :]).then_inc(psA_free, 1)

            def normalise1(b):
                act.wait_ge(ln1_ready, upto(b, 1, 1))
                for j in range(NT):
                    nc.scalar.activation(xn[:, j, :], x_in[:, j, :], ACT.Identity, bias=nmr1[:, j:j + 1],
                                         scale=rstd1[:, j:j + 1]).then_inc(xn_ready, 1)

            def keep_normed(b, first):
                if not first:
                    act.wait_ge(yc_ready, upto(b, 2, 0))
                act.wait_ge(xn_ready, upto(b, NT, NT))
                copy(xn_res[:], xn[:]).then_inc(xn_kept, 1)

            def project(b, first):
                for half in range(2):
                    evacuate(b, 0, half, xnT[:, bass.ts(half, HALF)])
                for half in range(2):
                    evacuate(b, 1, half, kT[:, PRE + half * HALF:PRE + (half + 1) * HALF])
                act.wait_ge(psA_free, upto(b, N_PSA_FREE, 4))
                nc.scalar.activation(kexp[:], kT[:, PRE:PRE + T], ACT.Exp)
                if not first:
                    act.wait_ge(conv_step, upto(b, N_CONV_STEPS, 0))
                for half in range(2):
                    evacuate(b, 2, half, vT[:, VPRE + half * HALF:VPRE + (half + 1) * HALF])
                nc.scalar.activation(fkT[:], kT[:, PRE:PRE + T], ACT.Relu).then_inc(k_feat, 1)
                for half in range(2):
                    evacuate(b, 3, half, qT[:, bass.ts(half, HALF)])
                act.wait_ge(psA_free, upto(b, N_PSA_FREE, 8))
                nc.scalar.activation(qexp[:], qT[:], ACT.Exp)
                nc.scalar.activation(fqT[:], qT[:], ACT.Relu).then_inc(q_feat, 1)

            def token_major(b):
                for half in range(2):
                    evacuate(b, 4, half, v_tok[:, half * TPH:(half + 1) * TPH, :].rearrange("p j c -> p (j c)"))
                for half in range(2):
                    evacuate(b, 5, half, fk_tok[:, half * TPH:(half + 1) * TPH, :].rearrange("p j c -> p (j c)"))

            def scores(b):
                for half in range(2):
                    evacuate(b, 6, half, scoresT[:, bass.ts(half, HALF)])

            def exponentials(b):
                act.wait_ge(logit_ready, upto(b, 1, 1))
                nc.scalar.activation(prob[:], logit[:], ACT.Exp, scale=float(HD) ** -0.5).then_inc(prob_ready, 1)

            def norm2(b):
                for j in range(NT):
                    if j % TPH == 0:
                        act.wait_ge(yc_ready, upto(b, 2, j // TPH + 1))
                    last = nc.scalar.activation(squares2[:, j, :], yc[:, j, :], ACT.Square, accum_out=ss2[:, j:j + 1])
                last.then_inc(ss2_ready, 1)

            def norm3_squares(b):
                for j in range(NT):
                    if j == 0:
                        act.wait_ge(mean_kept, upto(b, 1, 1))
                    act.wait_ge(x2_ready, upto(b, NT, j + 1))
                    last = nc.scalar.activation(squares3[:, j, :], x2[:, j, :], ACT.Square, bias=neg_mean3[:, j:j + 1],
                                                accum_out=ss3[:, j:j + 1])
                last.then_inc(ss3_ready, 1)

            def normalise3(b):
                act.wait_ge(ln3_ready, upto(b, 1, 1))
                for j in range(NT):
                    nc.scalar.activation(xn3[:, j, :], x2[:, j, :], ACT.Identity, bias=nmr3[:, j:j + 1],
                                         scale=rstd3[:, j:j + 1]).then_inc(xn3_ready, 1)

            def from_psF(b, use, rows, dst):
                act.wait_ge(psF_full, upto(b, N_PSF_FULL, use + 1))
                return copy(dst, psF[rows, use % 2, :])

            def gates(b):
                for half in range(2):
                    from_psF(b, half, slice(0, P), x3T[:, bass.ts(half, HALF)]).then_inc(psF_free, 1)
                for half in range(2):
                    from_psF(b, 2 + half, slice(0, P), gate_shared[:, bass.ts(half, HALF)]).then_inc(psF_free, 1)
                act.wait_ge(psF_full, upto(b, N_PSF_FULL, 5))
                nc.scalar.activation(gexp[:], psF[:, 0, 0:NT * EXPERTS].rearrange("p (j e) -> p j e", e=EXPERTS),
                                     ACT.Exp, scale=-1.0).then_inc(psF_free, 1)

            def hidden(b):
                nc.scalar.activation(hid[HID:P, 4, :], gate_shared[HID:P, :], ACT.Gelu, bias=bs1c[HID:P, :])
                for n in range(8):
                    c, half = n // 2, n % 2
                    act.wait_ge(psF_full, upto(b, N_PSF_FULL, 6 + n))
                    nc.scalar.activation(hid[:, c, bass.ts(half, HALF)], psF[:, (5 + n) % 2, :], ACT.Gelu,
                                         bias=b1c[:, c:c + 1]).then_inc(psF_free, 1)

            def spread_gates(b):
                act.wait_ge(psF_full, upto(b, N_PSF_FULL, 14))
                parts = psF[0:24, 1, :].bitcast(BF16)
                copy(gT[:], parts)
                copy(hid[0:24, 4, :], parts).then_inc(psF_free, 1)

            def norm4(b):
                for j in range(NT):
                    if j % TPH == 0:
                        act.wait_ge(psF_full, upto(b, N_PSF_FULL, 23 + j // TPH))
                    h, cols = bank(j)
                    last = nc.scalar.activation(squares4[:, j, :], psF[:, h, cols], ACT.Square, accum_out=ss4[:, j:j + 1])
                last.then_inc(ss4_ready, 1)

            normalise1(0)
            for b in range(B):
                first = b == 0
                project(b, first)
                keep_normed(b, first)
                if not first:
                    norm3_squares(b - 1)
                token_major(b)
                if not first:
                    normalise3(b - 1)
                    if b == 1:
                        act.wait_ge(ffn_ld, N_FFN_LD)
                    gates(b - 1)
                    hidden(b - 1)
                scores(b)
                if not first:
                    spread_gates(b - 1)
                exponentials(b)
                if not first:
                    norm4(b - 1)
                if b < B - 1:
                    normalise1(b + 1)
                norm2(b)
            norm3_squares(B - 1)
            normalise3(B - 1)
            gates(B - 1)
            hidden(B - 1)
            spread_gates(B - 1)
            norm4(B - 1)

        @block.vector
        def _(dve):
            nc.vector.memset(w1[:, 4 * P:5 * P], 0.0).then_inc(w_zeroed, 1)
            nc.vector.memset(w2[:, 4, :], 0.0).then_inc(w_zeroed, 1)
            nc.vector.memset(hid[0:32, 4, :], 1.0)
            nc.vector.memset(hid[32:HID, 4, :], 0.0)
            nc.vector.memset(ksum_sel[:], 0.0).then_inc(zeros_set, 1)

            def stats(b):
                dve.wait_ge(x_in_ld, upto(b, N_DMA, 16))
                for j in range(NT):
                    last = nc.vector.bn_stats(bn[:, j, :], x_in[:, j, :])
                last.then_inc(bn_done, 1)
                dve.wait_ge(bn_done, upto(b, 1, 1))
                for j in range(NT):
                    last = nc.vector.bn_aggr(mv[:, j, :], bn[:, j, :])
                last.then_inc(stats1, 1)

            def centre_weights():
                dve.wait_ge(consts_ready, 1)
                nc.vector.tensor_copy(identb[:], ident[:])
                dve.wait_ge(wo_ld, 16)
                nc.vector.tensor_reduce(row_mean[:, 0:1], wo[:], AX_X, ALU.add)
                dve.wait_ge(ffn_ld, N_FFN_LD)
                nc.vector.tensor_reduce(row_mean[:, 1:1 + CH], w2[:], AX_X, ALU.add).then_inc(w_means, 1)
                dve.wait_ge(w_means, 1)
                nc.vector.tensor_scalar(row_mean[:], row_mean[:], 1.0 / P, None, ALU.mult).then_inc(w_means, 1)
                dve.wait_ge(w_means, 2)
                nc.vector.tensor_scalar(wo[:], wo[:], row_mean[:, 0:1], None, ALU.subtract)
                nc.vector.tensor_tensor(w2[:], w2[:], row_mean[:, 1:1 + CH].unsqueeze(2).to_broadcast([P, CH, P]),
                                        ALU.subtract).then_inc(w_centred, 1)

            def key_features(b):
                dve.wait_ge(k_feat, upto(b, 1, 1))
                nc.vector.scalar_tensor_tensor(out=fkT[:], in0=kexp[:], scalar=1.0, in1=fkT[:], op0=ALU.min,
                                               op1=ALU.add, accum_out=ksum[:]).then_inc(fk_ready, 1)

            def query_features(b):
                dve.wait_ge(q_feat, upto(b, 1, 1))
                nc.vector.scalar_tensor_tensor(out=fqT[:], in0=qexp[:], scalar=1.0, in1=fqT[:], op0=ALU.min,
                                               op1=ALU.add).then_inc(fq_ready, 1)

            def products(b, s):
                if s == 0:
                    dve.wait_ge(psA_free, upto(b, N_PSA_FREE, 8))
                if s == 2:
                    dve.wait_ge(group_summed, upto(b, 2, 1))
                for q in range(QUADS):
                    off = TERMS[SLOTS * q + s]
                    if off == LOW:
                        continue
                    t0 = HALF if off == 512 else 0
                    nc.vector.tensor_tensor(prods[:, QUADS * (s % 2) + q, t0:T], qT[:, t0:T],
                                            kT[:, PRE - off + t0:PRE - off + T], ALU.mult).then_inc(prod_ready, 1)

            def linear_state(b):
                dve.wait_ge(fk_ready, upto(b, 1, 1))
                nc.vector.tensor_scalar(ksum_sel[:, 16:16 + HEADS], head_sel[:], ksum[:], None, ALU.mult)
                dve.wait_ge(kv_summed, upto(b, 1, 1))
                nc.vector.tensor_tensor(kv[:], psY[:, 0:P], head_mask[:], ALU.mult).then_inc(kv_ready, 1)

            def softmax_logits(b):
                dve.wait_ge(psA_full, upto(b, N_PSA_FULL, 16))
                softmax_chain.start(dve, b)
                pz = psA[:].rearrange("p a (j r) -> p (a j) r", r=P)
                z0 = 32 * (M_LOW // SLOTS) + HEADS * (M_LOW % SLOTS)
                nc.vector.tensor_scalar(zden[:], pz[:, :, z0:z0 + HEADS], 1e-6, None, ALU.add)
                for half in range(2):
                    ins = nc.vector.tensor_tensor(
                        logit[:, half * TPH:(half + 1) * TPH].rearrange("p j (q s) h -> p (j q) (s h)", s=SLOTS),
                        psA[:, half, :].rearrange("p (r c) -> p r c", c=32)[:, :, 0:SLOTS * HEADS],
                        mask[:, half * TPH:(half + 1) * TPH].rearrange("p j (q s) h -> p (j q) (s h)", s=SLOTS),
                        ALU.add)
                    ins.then_inc(scores_read, 1)
                dve.wait_ge(scores_read, upto(b, 2, 2))
                softmax_chain(nc.vector.tensor_reduce(top[:], logit[:].rearrange("p j m h -> p j h m"), AX_X, ALU.max))
                nc.vector.tensor_tensor(logit[:], logit[:], top[:].unsqueeze(2).to_broadcast([P, NT, NM, HEADS]),
                                        ALU.subtract).then_inc(logit_ready, 1)

            def softmax_weights(b):
                dve.wait_ge(prob_ready, upto(b, 1, 1))
                softmax_chain(nc.vector.tensor_reduce(den[:], prob[:].rearrange("p j m h -> p j h m"), AX_X, ALU.add))
                softmax_chain(nc.vector.reciprocal(rden[:], den[:]))
                softmax_chain(nc.vector.tensor_tensor(wgt[:], prob[:],
                                                      rden[:].unsqueeze(2).to_broadcast([P, NT, NM, HEADS]),
                                                      ALU.mult))
                softmax_chain(nc.vector.reciprocal(wgt[:, :, M_LOW, :], zden[:]))
                softmax_chain.done()

            def weigh(b, j):
                if j >= 2:
                    dve.wait_ge(terms_summed, upto(b, NT, j - 1))

                def term(m0, m1, src):
                    w = wgt[:, j, m0:m1, :].rearrange("p m h -> p (m h)").unsqueeze(2).to_broadcast(
                        [P, (m1 - m0) * HEADS, HD])
                    return nc.vector.tensor_tensor(
                        terms[:, j % 2, m0:m1, :].rearrange("p m (h d) -> p (m h) d", d=HD), src, w, ALU.mult)

                n = 1 + min(j // 2, 2)
                tiles = v_tok[:, j - 2 * (n - 1):j + 1:2, :].rearrange("p a (h d) -> p a h d", d=HD) if n > 1 else None
                if n == 1:
                    term(M_TILES + 2, M_TILES + 3, v_tok[:, j, :].rearrange("p (h d) -> p h d", d=HD))
                else:
                    m0 = M_TILES + 3 - n
                    w = wgt[:, j, m0:m0 + n, :].unsqueeze(3).to_broadcast([P, n, HEADS, HD])
                    nc.vector.tensor_tensor(
                        terms[:, j % 2, m0:m0 + n, :].rearrange("p m (h d) -> p m h d", d=HD), tiles, w, ALU.mult)
                if j >= 1:
                    term(M_128, M_128 + 1, v_tok[:, j - 1, :].rearrange("p (h d) -> p h d", d=HD))
                dve.wait_ge(shift1_ready, upto(b, NT, j + 1))
                term(0, 4, psG[:, 0, :].rearrange("p (a d) -> p a d", d=HD)).then_inc(shift1_used, 1)
                dve.wait_ge(shift2_ready, upto(b, NT, j + 1))
                term(4, 8, psG[:, 1, :].rearrange("p (a d) -> p a d", d=HD)).then_inc(terms_ready, 1)

            def add_conv(b, half):
                dve.wait_ge(terms_summed, upto(b, NT, TPH * (half + 1)))
                dve.wait_ge(conv_step, upto(b, N_CONV_STEPS, N_CONV_STEPS))
                cols = bass.ts(half, HALF)
                nc.vector.tensor_tensor(hT[:, cols], psH[:], convT[:, cols], ALU.add).then_inc(hT_ready, 1)

            def add_normed(b, half):
                dve.wait_ge(y_ready, upto(b, 2, half + 1))
                dve.wait_ge(xn_kept, upto(b, 1, 1))
                tiles = slice(half * TPH, (half + 1) * TPH)
                nc.vector.tensor_tensor(yc[:, tiles, :], psY[:].rearrange("p (j c) -> p j c", c=P),
                                        xn_res[:, tiles, :], ALU.add).then_inc(yc_ready, 1)

            def residual(b):
                dve.wait_ge(x_res_ld, upto(b, N_DMA, 16))
                dve.wait_ge(ln2_ready, upto(b, 1, 1))
                for j in range(NT):
                    nc.vector.scalar_tensor_tensor(out=x2[:, j, :], in0=yc[:, j, :], scalar=rstd2[:, j:j + 1],
                                                   in1=x_res[:, j, :], op0=ALU.mult, op1=ALU.add).then_inc(x2_ready, 1)

            def gates(b):
                bc = [P, NT, EXPERTS]
                den_, sig, score, eq, cand, one1, rest, one2, both, g = (t[:] for t in gtmp)
                m1, c1, m2, c2, msum, mrec = (t[:] for t in gmax)
                tt, ts = nc.vector.tensor_tensor, nc.vector.tensor_scalar
                dve.wait_ge(psF_free, upto(b, N_PSF_FREE, 5))
                ch = gate_chain
                ch.start(dve, b)
                ch(ts(den_, gexp[:], 1.0, None, ALU.add))
                ch(nc.vector.reciprocal(sig, den_))
                ch(ts(score, sig, rscale[:], None, ALU.mult))
                ch(nc.vector.tensor_reduce(m1, score, AX_X, ALU.max))
                ch(tt(eq, score, m1.unsqueeze(2).to_broadcast(bc), ALU.is_equal))
                ch(tt(cand, eq, first_pref[:], ALU.mult))
                ch(nc.vector.tensor_reduce(c1, cand, AX_X, ALU.max))
                ch(tt(one1, cand, c1.unsqueeze(2).to_broadcast(bc), ALU.is_equal))
                ch(nc.vector.scalar_tensor_tensor(out=rest, in0=one1, scalar=-BIG, in1=score, op0=ALU.mult,
                                                  op1=ALU.add))
                ch(nc.vector.tensor_reduce(m2, rest, AX_X, ALU.max))
                ch(tt(eq, rest, m2.unsqueeze(2).to_broadcast(bc), ALU.is_equal))
                ch(tt(cand, eq, first_pref[:], ALU.mult))
                ch(nc.vector.tensor_reduce(c2, cand, AX_X, ALU.max))
                ch(tt(one2, cand, c2.unsqueeze(2).to_broadcast(bc), ALU.is_equal))
                ch(tt(both, one1, one2, ALU.add))
                ch(tt(both, both, score, ALU.mult))
                ch(tt(msum, m1, m2, ALU.add))
                ch(nc.vector.reciprocal(mrec, msum))
                ch(tt(g, both, mrec.unsqueeze(2).to_broadcast(bc), ALU.mult))
                ch(nc.vector.tensor_copy(gparts[:, :, 0, :], g))
                ch(tt(rest, g, gparts[:, :, 0, :], ALU.subtract))
                ch(nc.vector.tensor_copy(gparts[:, :, 1, :], rest))
                ch(tt(cand, rest, gparts[:, :, 1, :], ALU.subtract))
                ch(nc.vector.tensor_copy(gparts[:, :, 2, :], cand))
                ch.done()

            def gate_hidden(b):
                for n in range(8):
                    c, half = n // 2, n % 2
                    cols = bass.ts(half, HALF)
                    dve.wait_ge(psF_full, upto(b, N_PSF_FULL, 15 + n))
                    nc.vector.tensor_tensor(hid[:, c, cols], hid[:, c, cols], psF[:, n % 2, :],
                                            ALU.mult).then_inc(gated, 1)

            def finish(b, first):
                if not first:
                    dve.wait_ge(out_stored, upto(b, N_DMA, 0))
                dve.wait_ge(ln4_ready, upto(b, 1, 1))
                for j in range(NT):
                    h, cols = bank(j)
                    nc.vector.scalar_tensor_tensor(out=y_out[:, j, :], in0=psF[:, h, cols], scalar=rstd4[:, j:j + 1],
                                                   in1=x2[:, j, :], op0=ALU.mult, op1=ALU.add).then_inc(out_ready, 1)

            stats(0)
            dve.wait_ge(consts_ready, 1)
            dve.wait_ge(zeros_set, 1)
            for b in range(B):
                first = b == 0
                if not first:
                    residual(b - 1)
                key_features(b)
                products(b, 0)
                linear_state(b)
                query_features(b)
                products(b, 1)
                products(b, 2)
                if first:
                    centre_weights()
                else:
                    gates(b - 1)
                softmax_logits(b)
                if not first:
                    gate_hidden(b - 1)
                softmax_weights(b)
                for j in range(NT):
                    weigh(b, j)
                    if j == 2 and b < B - 1:
                        stats(b + 1)
                    if j == TPH:
                        add_conv(b, 0)
                    if j == TPH + 1:
                        add_normed(b, 0)
                    if j == TPH + 2 and not first:
                        finish(b - 1, b == 1)
                add_conv(b, 1)
                add_normed(b, 1)
            residual(B - 1)
            gates(B - 1)
            gate_hidden(B - 1)
            finish(B - 1, False)

        @block.tensor
        def _(pe):
            def claim_psA(b, use, half, first):
                if use:
                    pe.wait_ge(psA_free, upto(b, N_PSA_FREE, 2 * (use - 1) + half + 1))
                elif not first:
                    pe.wait_ge(scores_read, upto(b, 2, half - 1))

            def turn(b, use, src, first):
                for j in range(NT):
                    h, cols = bank(j)
                    if j % TPH == 0:
                        claim_psA(b, use, h, first)
                    ins = pe.transpose(psA[:, h, cols], src(j), ident[:])
                    if j % TPH == TPH - 1:
                        ins.then_inc(psA_full, 1)

            def project(b, first):
                pe.wait_ge(xn_ready, upto(b, NT, NT))
                turn(b, 0, lambda j: xn[:, j, :], first)
                for use, part in ((1, 1), (2, 2), (3, 0)):
                    for half in range(2):
                        claim_psA(b, use, half, first)
                        pe.matmul(psA[:, half, :], wqkv[:, bass.ts(part, P)], xnT[:, bass.ts(half, HALF)],
                                  start=True, stop=True).then_inc(psA_full, 1)

            def token_major(b):
                turn(b, 4, lambda j: vT[:, VPRE + j * P:VPRE + (j + 1) * P], False)
                pe.wait_ge(fk_ready, upto(b, 1, 1))
                turn(b, 5, lambda j: fkT[:, bass.ts(j, P)], False)

            def linear_state(b, first):
                if not first:
                    pe.wait_ge(yc_ready, upto(b, 2, 0))
                pe.wait_ge(psA_free, upto(b, N_PSA_FREE, 12))
                for j in range(NT):
                    ins = pe.matmul(psY[:, 0:P], fk_tok[:, j, :], v_tok[:, j, :], start=(j == 0), stop=(j == NT - 1))
                ins.then_inc(kv_summed, 1)

            def sum_heads(b, s):
                pe.wait_ge(prod_ready, upto(b, N_PRODUCTS, min(4 * (s + 1), N_PRODUCTS)))
                if s == 2:
                    pe.wait_ge(fq_ready, upto(b, 1, 1))
                    pe.wait_ge(kv_ready, upto(b, 1, 1))
                for half in range(2):
                    if s == 0:
                        claim_psA(b, 6, half, False)
                    cols = bass.ts(half, HALF)
                    for q in range(QUADS):
                        off = TERMS[SLOTS * q + s]
                        none = off == 512 and half == 0
                        if none:
                            continue
                        low = off == LOW
                        last = s == 2 or (TERMS[SLOTS * q + 2] == 512 and half == 0 and s == 1)
                        ins = pe.matmul(psA[32 * q:32 * q + 32, half, :], ksum_sel[:] if low else slot_sel[:, s, :],
                                        fqT[:, cols] if low else prods[:, QUADS * (s % 2) + q, cols],
                                        start=(s == 0), stop=last)
                    if s == 2:
                        ins.then_inc(psA_full, 1)
                if s < 2:
                    ins.then_inc(group_summed, 1)

            def turn_scores(b):
                turn(b, 7, lambda j: scoresT[:, bass.ts(j, P)], False)

            def shift(b, j, first):
                if not (first and j == 0):
                    pe.wait_ge(shift1_used, upto(b, NT, j))
                for m in range(4):
                    t = VPRE + j * P - TERMS[m]
                    ins = pe.transpose(psG[:, 0, bass.ts(m, P)], vT[:, t:t + P], ident[:])
                ins.then_inc(shift1_ready, 1)
                if not (first and j == 0):
                    pe.wait_ge(terms_ready, upto(b, NT, j))
                for m in range(4, 8):
                    dst = psG[:, 1, bass.ts(m - 4, P)]
                    if TERMS[m] == LOW:
                        ins = pe.matmul(dst, fqT[:, bass.ts(j, P)], kv[:], start=True, stop=True)
                    else:
                        t = VPRE + j * P - TERMS[m]
                        ins = pe.transpose(dst, vT[:, t:t + P], ident[:])
                ins.then_inc(shift2_ready, 1)

            def sum_terms(b, j, first):
                pe.wait_ge(terms_ready, upto(b, NT, j + 1))
                if j % TPH == 0 and not (first and j == 0):
                    pe.wait_ge(hT_ready, upto(b, 2, j // TPH))
                live = [m for m, off in enumerate(TERMS) if off < P or off // P <= j]
                for m in live:
                    ins = pe.matmul(psH[:, bass.ts(j % TPH, P)], terms[:, j % 2, m, :], ident[:], is_transpose=True,
                                    start=(m == live[0]), stop=(m == live[-1]))
                ins.then_inc(terms_summed, 1)

            def output(b, half):
                pe.wait_ge(hT_ready, upto(b, 2, half + 1))
                if half:
                    pe.wait_ge(yc_ready, upto(b, 2, 1))
                for j in range(TPH * half, TPH * (half + 1)):
                    ins = pe.matmul(psY[:, bass.ts(j % TPH, P)], hT[:, bass.ts(j, P)], wo[:], start=True, stop=True)
                ins.then_inc(y_ready, 1)

            def gates(b, first):
                pe.wait_ge(xn3_ready, upto(b, NT, NT))
                for j in range(NT):
                    h, cols = bank(j)
                    if j % TPH == 0 and not first:
                        pe.wait_ge(out_ready, upto(b, NT, TPH * (h - 1)))
                    ins = pe.transpose(psF[:, h, cols], xn3[:, j, :], ident[:])
                    if j % TPH == TPH - 1:
                        ins.then_inc(psF_full, 1)
                for half in range(2):
                    pe.wait_ge(psF_free, upto(b, N_PSF_FREE, half + 1))
                    pe.matmul(psF[:, half, :], w1[:, 4 * P:5 * P], x3T[:, bass.ts(half, HALF)],
                              start=True, stop=True).then_inc(psF_full, 1)
                pe.wait_ge(psF_free, upto(b, N_PSF_FREE, 4))
                for j in range(NT):
                    ins = pe.transpose(psF[:, 0, bass.ts(j, EXPERTS)], gate_shared[0:EXPERTS, bass.ts(j, P)],
                                       ident[0:EXPERTS, 0:EXPERTS])
                ins.then_inc(psF_full, 1)

            def hidden(b):
                for n in range(8):
                    c, half = n // 2, n % 2
                    pe.wait_ge(psF_free, upto(b, N_PSF_FREE, max(4, 4 + n)))
                    pe.matmul(psF[:, (5 + n) % 2, :], w1[:, bass.ts(c, P)], x3T[:, bass.ts(half, HALF)],
                              start=True, stop=True).then_inc(psF_full, 1)

            def spread_gates(b):
                pe.wait_ge(gate_step, upto(b, N_GATE_STEPS, N_GATE_STEPS))
                pe.wait_ge(psF_free, upto(b, N_PSF_FREE, 12))
                parts = psF[0:24, 1, :].bitcast(BF16)
                for j in range(NT):
                    ins = pe.transpose(parts[:, bass.ts(j, P)], gparts[:, j].rearrange("p a e -> p (a e)"), identb[:])
                ins.then_inc(psF_full, 1)
                for n in range(8):
                    c, half = n // 2, n % 2
                    if n == 0:
                        pe.wait_ge(psF_free, upto(b, N_PSF_FREE, 14))
                    if n >= 2:
                        pe.wait_ge(gated, upto(b, 8, n - 1))
                    pe.matmul(psF[:, n % 2, :], gate_sel[:, c, :], gT[:, bass.ts(half, HALF)],
                              start=True, stop=True).then_inc(psF_full, 1)

            def experts_out(b):
                for j in range(NT):
                    h, cols = bank(j)
                    if j == 0:
                        pe.wait_ge(gated, upto(b, 8, 8))
                    for c in range(CH):
                        ins = pe.matmul(psF[:, h, cols], hid[:, c, bass.ts(j, P)], w2[:, c, :],
                                        start=(c == 0), stop=(c == CH - 1))
                    if j % TPH == TPH - 1:
                        ins.then_inc(psF_full, 1)

            pe.wait_ge(consts_ready, 1)
            pe.wait_ge(wqkv_ld, 16)
            for b in range(B):
                first = b == 0
                project(b, first)
                token_major(b)
                linear_state(b, first)
                sum_heads(b, 0)
                if not first:
                    gates(b - 1, b == 1)
                sum_heads(b, 1)
                if not first:
                    hidden(b - 1)
                sum_heads(b, 2)
                turn_scores(b)
                if not first:
                    spread_gates(b - 1)
                    experts_out(b - 1)
                for j in range(NT):
                    shift(b, j, first)
                    if j:
                        sum_terms(b, j - 1, first)
                    if first and j == TPH:
                        pe.wait_ge(w_centred, 1)
                    if j == TPH + 1:
                        output(b, 0)
                sum_terms(b, NT - 1, first)
                output(b, 1)
            gates(B - 1, False)
            hidden(B - 1)
            spread_gates(B - 1)
            experts_out(B - 1)


_INS = ['L0_attn_x', 'L0_attn_Wqkv', 'L0_attn_Wo', 'L0_attn_conv_w', 'L0_ffn_gate_W', 'L0_ffn_W1', 'L0_ffn_b1',
        'L0_ffn_W2', 'L0_ffn_b2', 'L0_ffn_Ws1', 'L0_ffn_bs1', 'L0_ffn_Ws2', 'L0_ffn_bs2', 'L0_ffn_route_scale']


def kernel(**inputs):
    import concourse.bacc as bacc
    from concourse.bass_utils import run_bass_kernel_spmd

    nc = bacc.Bacc("TRN2", target_bir_lowering=False, num_devices=1)
    arrays, args = {}, []
    for name in _INS:
        a = np.ascontiguousarray(inputs[name])
        if a.ndim == 0:
            a = a.reshape(1)
        arrays[name] = a
        args.append(nc.dram_tensor(name, a.shape, mybir.dt.from_np(a.dtype), kind="ExternalInput").ap())
    shape = inputs['L0_attn_x'].shape
    args.append(nc.dram_tensor("out", shape, F32, kind="ExternalOutput").ap())
    block_kernel(nc, *args)
    r = run_bass_kernel_spmd(nc, [arrays], core_ids=[0])
    return r.results[0]["out"]
```

```python
from contextlib import ExitStack

import numpy as np

import concourse.bass as bass
from concourse import mybir

F32 = mybir.dt.float32
BF16 = mybir.dt.bfloat16
ALU = mybir.AluOpType
ACT = mybir.ActivationFunctionType
AX_X = mybir.AxisListType.X

P = 128
HEADS = 8
HD = P // HEADS
TAPS = 7
EXPERTS = 8
HID = 64
T = 1024
NT = T // P
HALF = 512
TPH = HALF // P
EPS = 1e-5
BIG = 3.0e38
PRE = 512
VPRE = 64

LOW = -1
TERMS = [128, 512, 256, 0, 1, 2, 4, 8, 16, 32, 64, LOW]
NM = len(TERMS)
M_LOW = TERMS.index(LOW)
M_128 = TERMS.index(128)
M_TILES = TERMS.index(512)
M_SHIFT = TERMS.index(1)
SHIFTS = TERMS[M_SHIFT:M_LOW]
NV = M_LOW
SLOTS, QUADS = 3, 4
POOL_PRODUCTS = ((1, 0), (1, 1), (2, 0))
TERM_BUFS = 4
CH = 5

N_DMA = 16
N_SHIFT_DMA = 16 * 2 * len(SHIFTS)
N_PSA_FULL, N_PSA_FREE = 16, 14
PSA_V_TOK, PSA_FK_TOK, PSA_SCORES, PSA_SCORES_T, PSA_X, PSA_K, PSA_Q, PSA_V = range(8)
PSA_AHEAD = 2 * 4
N_PRODUCTS = (4, 6, 8)
N_SOFTMAX_STEPS = 5
N_CONV_STEPS = 2 * TAPS - 1
N_FRONT = 3
N_HIDDEN = 4
X3, C4, LOGITS = range(N_FRONT)
N_GATE_STEPS = 24


def upto(b, per_batch, n):
    return b * per_batch + n


def filled(b, use, half):
    return upto(b, N_PSA_FULL, PSA_AHEAD + 2 * use + half + 1)


def psF_fill(u, use):
    return upto(u // 2, 2 * (N_FRONT + N_HIDDEN) + 1, (N_FRONT + N_HIDDEN) * (u % 2) + use)


def freed(b, use, half):
    return upto(b, N_PSA_FREE, PSA_AHEAD + 2 * (use - (use > PSA_SCORES_T)) + half + 1)


class Chain:

    def __init__(self, sem, per_batch):
        self.sem, self.per_batch = sem, per_batch

    def start(self, eng, b):
        self.eng, self.b, self.n = eng, b, 0

    def __call__(self, ins):
        self.n += 1
        ins.then_inc(self.sem, 1)
        self.eng.wait_ge(self.sem, upto(self.b, self.per_batch, self.n))

    def done(self):
        assert self.n == self.per_batch, (self.n, self.per_batch)


def block_kernel(nc, x, Wqkv, Wo, conv_w, gate_W, W1, b1, W2, b2, Ws1, bs1, Ws2, bs2, route_scale, out):
    B = x.shape[0]
    x_tok = x.rearrange("b (j p) c -> b p j c", p=P)
    out_tok = out.rearrange("b (j p) c -> b p j c", p=P)

    with ExitStack() as ctx:
        def sb(name, shape, dt=F32):
            return ctx.enter_context(nc.sbuf_tensor(name, shape, dt))

        def psum(name, shape, dt=F32):
            return ctx.enter_context(nc.psum_tensor(name, shape, dt))

        def sem(name):
            return ctx.enter_context(nc.semaphore(name))

        ctx.enter_context(nc.allow_non_contiguous_dma(reason="small bias vectors"))

        ident = sb("ident", [P, P])
        identb = sb("identb", [P, P], BF16)
        head_sel = sb("head_sel", [P, HEADS])
        head_mask = sb("head_mask", [P, P])
        slot_sel = sb("slot_sel", [P, SLOTS, 32])
        ksum_sel = sb("ksum_sel", [P, 32])
        mask = sb("mask", [P, NT, NM, HEADS])
        first_pref = sb("first_pref", [P, TPH, EXPERTS])
        gate_sel = sb("gate_sel", [24, 4, P], BF16)
        neg_half = sb("neg_half", [P, NT])
        wqkv = sb("wqkv", [P, 3 * P])
        wo = sb("wo", [P, P])
        cw = sb("cw", [P, TAPS])
        w1 = sb("w1", [P, CH * P])
        w2 = sb("w2", [P, CH, P])
        b1c = sb("b1c", [P, 4])
        bs1c = sb("bs1c", [P, 1])
        rscale = sb("rscale", [P, 1])
        row_mean = sb("row_mean", [P, 1 + CH])

        x_in = sb("x_in", [P, NT, P])
        x_res = sb("x_res", [P, NT, P])
        xn = sb("xn", [P, NT, P])
        xn_res = sb("xn_res", [P, NT, P])
        yc = sb("yc", [P, NT, P])
        x2 = sb("x2", [P, NT, P])
        xn3 = sb("xn3", [P, NT, P])
        fk_tok = sb("fk_tok", [P, NT, P])
        v_tok = sb("v_tok", [P, NT, P])
        bn = sb("bn", [P, NT, 6])
        mv = sb("mv", [P, NT, 2])
        neg_mean = sb("neg_mean", [P, 3, NT])
        var1, rstd1, nmr1 = sb("var1", [P, NT]), sb("rstd1", [P, NT]), sb("nmr1", [P, NT])
        ss2, var2, rstd2 = sb("ss2", [P, NT]), sb("var2", [P, NT]), sb("rstd2", [P, NT])
        ss3, var3, rstd3, nmr3 = sb("ss3", [P, NT]), sb("var3", [P, NT]), sb("rstd3", [P, NT]), sb("nmr3", [P, NT])
        ss4, var4, rstd4 = sb("ss4", [P, NT]), sb("var4", [P, NT]), sb("rstd4", [P, NT])
        squares, squares4 = sb("squares", [P, NT, P]), sb("squares4", [P, NT, P])
        logit = sb("logit", [P, NT, NM, HEADS])
        top = sb("top", [P, NT, HEADS])
        prob = sb("prob", [P, NT, NM, HEADS])
        den = sb("den", [P, NT, HEADS])
        rden = sb("rden", [P, NT, HEADS])
        zden = sb("zden", [P, NT, HEADS])
        wgt = sb("wgt", [P, NT, NM, HEADS])
        v_shift = sb("v_shift", [P, len(SHIFTS), NT, P])

        xnT = sb("xnT", [P, T])
        kT = sb("kT", [P, PRE + T])
        vT = sb("vT", [P, VPRE + T])
        qT = sb("qT", [P, T])
        kexp, fkT = sb("kexp", [P, T]), sb("fkT", [P, T])
        qexp, fqT = sb("qexp", [P, T]), sb("fqT", [P, T])
        ksum = sb("ksum", [P, 1])
        kv = sb("kv", [P, P])
        prods = sb("prods", [P, 2 * QUADS, T])
        convT = sb("convT", [P, T])
        tapT = sb("tapT", [P, T])
        space = prods[:].rearrange("p a t -> p (a t)")
        n_terms = TERM_BUFS * NV * P
        terms = space[:, 0:n_terms].rearrange("p (a m c) -> p a m c", a=TERM_BUFS, m=NV)
        low_terms = space[:, n_terms:n_terms + T].rearrange("p (j c) -> p j c", c=P)
        hT = space[:, n_terms + T:n_terms + 2 * T]
        scoresT = space[:, 7 * T:8 * T]
        assert n_terms + 2 * T <= 8 * T

        x3T = sb("x3T", [P, T])
        gate_shared = sb("gate_shared", [P, T])
        gexp = sb("gexp", [P, TPH, EXPERTS])
        gtmp = [sb(f"gtmp{i}", [P, TPH, EXPERTS]) for i in range(10)]
        gmax = [sb(f"gmax{i}", [P, TPH]) for i in range(6)]
        gparts = sb("gparts", [P, TPH, 3, EXPERTS], BF16)
        gT = sb("gT", [24, HALF], BF16)
        hid = sb("hid", [P, CH, T])
        y_out = sb("y_out", [P, NT, P])

        psA = psum("psA", [P, 2, HALF])
        psG = psum("psG", [P, 2, HALF])
        psH = psum("psH", [P, HALF])
        psY = psum("psY", [P, HALF])
        psF = psum("psF", [P, 2, HALF])

        wqkv_ld, conv_ld, wo_ld, ffn_ld = sem("wqkv_ld"), sem("conv_ld"), sem("wo_ld"), sem("ffn_ld")
        x_in_ld, x_res_ld, out_stored = sem("x_in_ld"), sem("x_res_ld"), [sem(f"out_stored{h}") for h in range(2)]
        pool_set, zeros_set, consts_ready = sem("pool_set"), sem("zeros_set"), sem("consts_ready")
        ident_ready = sem("ident_ready")
        w_zeroed, w_means, w_centred = sem("w_zeroed"), sem("w_means"), sem("w_centred")
        stats1 = sem("stats1")
        bn_done = sem("bn_done")
        ln1_ready, ln2_ready, ln3_ready, ln4_ready = sem("ln1_ready"), sem("ln2_ready"), sem("ln3_ready"), sem("ln4_ready")
        ln1_step, ln2_step, ln3_step, ln4_step = sem("ln1_step"), sem("ln2_step"), sem("ln3_step"), sem("ln4_step")
        xn_ready, xn_kept = sem("xn_ready"), sem("xn_kept")
        psA_full, psA_free, scores_read = sem("psA_full"), sem("psA_free"), sem("scores_read")
        k_feat, q_feat = sem("k_feat"), sem("q_feat")
        fk_ready, fq_ready = sem("fk_ready"), sem("fq_ready")
        kv_summed, kv_ready = sem("kv_summed"), sem("kv_ready")
        prod_ready, group_summed = sem("prod_ready"), sem("group_summed")
        logit_ready, prob_ready, softmax_step = sem("logit_ready"), sem("prob_ready"), sem("softmax_step")
        v_shifted, low_ready, low_used = sem("v_shifted"), sem("low_ready"), sem("low_used")
        pool_prod_ready = sem("pool_prod_ready")
        terms_ready, terms_summed = sem("terms_ready"), sem("terms_summed")
        conv_step, hT_ready, y_ready, yc_ready = sem("conv_step"), sem("hT_ready"), sem("y_ready"), sem("yc_ready")
        ss2_ready, x2_ready, ss3_ready, xn3_ready = sem("ss2_ready"), sem("x2_ready"), sem("ss3_ready"), sem("xn3_ready")
        front_full, front_free = sem("front_full"), sem("front_free")
        hidden_full, hidden_free = sem("hidden_full"), sem("hidden_free")
        gates_turned = sem("gates_turned")
        gate_spread, gated = sem("gate_spread"), sem("gated")
        gate_step, gT_ready, experts_summed = sem("gate_step"), sem("gT_ready"), sem("experts_summed")
        ss4_ready, out_ready = sem("ss4_ready"), sem("out_ready")

        softmax_chain = Chain(softmax_step, N_SOFTMAX_STEPS)
        conv_chain = Chain(conv_step, N_CONV_STEPS)

        def bank(tile):
            return tile // TPH, bass.ts(tile % TPH, P)

        def product(eng, s, q):
            off = TERMS[SLOTS * q + s]
            t0 = HALF if off == 512 else 0
            return eng.tensor_tensor(prods[:, QUADS * (s % 2) + q, t0:T], qT[:, t0:T],
                                     kT[:, PRE - off + t0:PRE - off + T], ALU.mult)

        def x2_of(u):
            return x2[:] if u < 2 * B - 2 else qexp[:].rearrange("p (j c) -> p j c", c=P)

        def front(u, use):
            if u < 2 * B - 2:
                return psF[:, psF_fill(u, use) % 2, :]
            return psY[:] if use == C4 else psH[:]

        def hidden_bank(u, c):
            return psF[:, psF_fill(u, N_FRONT + c) % 2, :]

        def outputs(u):
            if u < 2 * B - 3:
                return psF[:, psF_fill(u, N_FRONT + N_HIDDEN) % 2, :] if u % 2 else psY[:]
            return psA[:, u % 2, :]

        block = ctx.enter_context(nc.Block())

        @block.sync
        def _(sp):
            sp.dma_start(x_in[:], x_tok[0]).then_inc(x_in_ld, 16)
            sp.dma_start(wqkv[:], Wqkv).then_inc(wqkv_ld, 16)
            sp.dma_start(cw[:], conv_w).then_inc(conv_ld, 16)
            sp.dma_start(wo[:], Wo).then_inc(wo_ld, 16)
            sp.dma_start(x_res[:], x_tok[0]).then_inc(x_res_ld, 16)
            sp.wait_ge(w_zeroed, 2)
            sp.dma_start(w1[:, 0:EXPERTS * HID].rearrange("d (e h) -> d e h", e=EXPERTS),
                         W1.rearrange("e d h -> d e h")).then_inc(ffn_ld, 16)
            sp.dma_start(w1[:, 4 * P:4 * P + EXPERTS], gate_W).then_inc(ffn_ld, 16)
            sp.dma_start(w1[:, 4 * P + HID:5 * P], Ws1).then_inc(ffn_ld, 16)
            sp.dma_start(w2[:, 0:4, :], W2.rearrange("(c e) h n -> (e h) c n", e=2)).then_inc(ffn_ld, 16)
            for part in range(3):
                sp.dma_start(w2[8 * part:8 * part + 8, 4, :], b2).then_inc(ffn_ld, 16)
            sp.dma_start(w2[24:25, 4, :], bs2.rearrange("(a n) -> a n", a=1)).then_inc(ffn_ld, 16)
            sp.dma_start(w2[HID:P, 4, :], Ws2).then_inc(ffn_ld, 16)
            sp.dma_start(b1c[:], b1.rearrange("(c e) h -> (e h) c", e=2)).then_inc(ffn_ld, 16)
            sp.dma_start(bs1c[HID:P, :], bs1.rearrange("(h a) -> h a", a=1)).then_inc(ffn_ld, 16)
            sp.dma_start(rscale[:], route_scale.rearrange("(a n) -> a n", a=1).to_broadcast([P, 1])).then_inc(ffn_ld, 16)

            def load_next(b):
                sp.wait_ge(xn_ready, upto(b, NT, NT))
                sp.dma_start(x_in[:], x_tok[b + 1]).then_inc(x_in_ld, 16)

            def load_residual(b):
                sp.wait_ge(x2_ready, upto(b, NT, 0))
                sp.dma_start(x_res[:], x_tok[b]).then_inc(x_res_ld, 16)

            def shift_v(b):
                sp.wait_ge(psA_free, freed(b, PSA_V_TOK, 1))
                for n, off in enumerate(SHIFTS):
                    sp.dma_start(v_shift[off:P, n], v_tok[0:P - off]).then_inc(v_shifted, 16)
                    sp.dma_start(v_shift[0:off, n, 1:NT], v_tok[P - off:P, 0:NT - 1]).then_inc(v_shifted, 16)

            def store(u):
                sp.wait_ge(out_ready, upto(u, TPH, TPH))
                tiles = slice(u % 2 * TPH, (u % 2 + 1) * TPH)
                sp.dma_start(out_tok[u // 2][:, tiles], y_out[:, tiles]).then_inc(out_stored[u % 2], 16)

            for b in range(B + 1):
                if b < B - 1:
                    load_next(b)
                if b < B:
                    shift_v(b)
                if b >= 2:
                    store(2 * b - 3)
                if 1 <= b < B:
                    load_residual(b)
                if b:
                    store(2 * b - 2)
            store(2 * B - 1)
            for half in range(2):
                sp.wait_ge(out_stored[half], upto(B, N_DMA, 0))

        N_FFN_LD = 16 * 12

        @block.gpsimd
        def _(pool):
            nc.gpsimd.memset(neg_half[:], -0.5)
            nc.gpsimd.memset(ident[:], 0.0)
            nc.gpsimd.memset(head_sel[:], 1.0)
            nc.gpsimd.memset(head_mask[:], 1.0)
            nc.gpsimd.memset(slot_sel[:], 0.0)
            nc.gpsimd.memset(gate_sel[:], 0.0)
            nc.gpsimd.memset(mask[:], 0.0).then_inc(pool_set, 1)
            pool.wait_ge(pool_set, 1)
            nc.gpsimd.affine_select(out=ident[:], in_=ident[:], compare_op=ALU.not_equal, fill=1.0, base=0,
                                    pattern=[[-1, P]], channel_multiplier=1).then_inc(ident_ready, 1)

            def constants():
                nc.gpsimd.affine_select(out=head_sel[:], in_=head_sel[:], compare_op=ALU.is_ge, fill=0.0, base=0,
                                        pattern=[[-HD, HEADS]], channel_multiplier=1)
                v = head_mask[:].rearrange("p (h d) -> p h d", h=HEADS)
                nc.gpsimd.affine_select(out=v, in_=v, compare_op=ALU.is_ge, fill=0.0, base=0,
                                        pattern=[[-HD, HEADS], [0, HD]], channel_multiplier=1).then_inc(pool_set, 1)
                pool.wait_ge(pool_set, 2)
                nc.gpsimd.affine_select(out=head_sel[:], in_=head_sel[:], compare_op=ALU.is_ge, fill=0.0, base=HD - 1,
                                        pattern=[[HD, HEADS]], channel_multiplier=-1)
                nc.gpsimd.affine_select(out=v, in_=v, compare_op=ALU.is_ge, fill=0.0, base=HD - 1,
                                        pattern=[[HD, HEADS], [0, HD]], channel_multiplier=-1).then_inc(pool_set, 1)
                pool.wait_ge(pool_set, 3)
                for s in range(SLOTS):
                    nc.gpsimd.tensor_copy(slot_sel[:, s, HEADS * s:HEADS * s + HEADS], head_sel[:])
                nc.gpsimd.memset(kT[:, 0:PRE], 0.0)
                nc.gpsimd.memset(vT[:, 0:VPRE], 0.0).then_inc(consts_ready, 1)

            def more_constants():
                for m, off in enumerate(TERMS):
                    v = mask[:, :, m, :]
                    if off == LOW:
                        nc.gpsimd.memset(v, -BIG)
                    else:
                        nc.gpsimd.affine_select(out=v, in_=v, compare_op=ALU.is_ge, fill=-BIG, base=-off,
                                                pattern=[[P, NT], [0, HEADS]], channel_multiplier=1)
                for n, off in enumerate(SHIFTS):
                    nc.gpsimd.memset(v_shift[0:off, n, 0, :], 0.0)
                for e in range(EXPERTS):
                    nc.gpsimd.memset(first_pref[:, :, e:e + 1], float(EXPERTS - e))
                for part in range(3):
                    v = gate_sel[:].rearrange("r c (a n) -> r c a n", a=2)
                    nc.gpsimd.affine_select(out=v, in_=v, compare_op=ALU.not_equal, fill=1.0, base=-EXPERTS * part,
                                            pattern=[[-2, 4], [-1, 2], [0, HID]],
                                            channel_multiplier=1).then_inc(pool_set, 1)
                    pool.wait_ge(pool_set, 4 + part)
                nc.gpsimd.memset(neg_half[0:1, 0:1], -0.5).then_inc(consts_ready, 1)

            def rstd_of(var, src, scale, rstd, step, value, cols):
                nc.gpsimd.tensor_scalar(var[:, cols], src, scale, EPS, ALU.mult, ALU.add).then_inc(step, 1)
                pool.wait_ge(step, value)
                return nc.gpsimd.tensor_tensor(rstd[:, cols], var[:, cols], neg_half[:, cols], ALU.pow)

            def ln1(b):
                pool.wait_ge(stats1, upto(b, 1, 1))
                if b >= 3:
                    pool.wait_ge(ln3_ready, 2 * (b - 2))
                nc.gpsimd.tensor_scalar(neg_mean[:, b % 3, :], mv[:, :, 0], -1.0, 0.0, ALU.mult, ALU.add)
                rstd_of(var1, mv[:, :, 1], 1.0, rstd1, ln1_step, upto(b, 2, 1), slice(0, NT)).then_inc(ln1_step, 1)
                pool.wait_ge(ln1_step, upto(b, 2, 2))
                nc.gpsimd.tensor_tensor(nmr1[:], neg_mean[:, b % 3, :], rstd1[:], ALU.mult).then_inc(ln1_ready, 1)

            def products(b, slots):
                for s in slots:
                    if s == 1:
                        pool.wait_ge(psA_free, freed(b - 1, PSA_Q, 1))
                        pool.wait_ge(y_ready, upto(b, 2, 0))
                    else:
                        pool.wait_ge(group_summed, upto(b, 2, 1))
                    for q in range(QUADS):
                        if (s, q) in POOL_PRODUCTS:
                            product(nc.gpsimd, s, q).then_inc(pool_prod_ready, 1)

            def conv_start(b):
                pool.wait_ge(psA_free, freed(b - 1, PSA_V, 1))
                if b == 0:
                    pool.wait_ge(conv_ld, 16)
                else:
                    pool.wait_ge(hT_ready, upto(b, 2, 0))
                conv_chain.start(pool, b)
                conv_chain(nc.gpsimd.tensor_scalar(convT[:], vT[:, VPRE:VPRE + T], cw[:, TAPS - 1:TAPS], 0.0,
                                                   ALU.mult, ALU.add))

            def conv_taps(b, shifts):
                for shift in shifts:
                    conv_chain(nc.gpsimd.tensor_scalar(tapT[:], vT[:, VPRE - shift:VPRE - shift + T],
                                                       cw[:, TAPS - 1 - shift:TAPS - shift], 0.0,
                                                       ALU.mult, ALU.add))
                    conv_chain(nc.gpsimd.tensor_tensor(convT[:], convT[:], tapT[:], ALU.add))

            def ln2(u):
                pool.wait_ge(ss2_ready, u + 1)
                cols = slice(u % 2 * TPH, (u % 2 + 1) * TPH)
                rstd_of(var2, ss2[:, cols], 1.0 / P, rstd2, ln2_step, u + 1, cols).then_inc(ln2_ready, 1)

            def ln3(u):
                pool.wait_ge(ss3_ready, u + 1)
                cols = slice(u % 2 * TPH, (u % 2 + 1) * TPH)
                rstd_of(var3, ss3[:, cols], 1.0 / P, rstd3, ln3_step, upto(u, 2, 1), cols).then_inc(ln3_step, 1)
                pool.wait_ge(ln3_step, upto(u, 2, 2))
                nc.gpsimd.tensor_tensor(nmr3[:, cols], neg_mean[:, u // 2 % 3, cols], rstd3[:, cols],
                                        ALU.mult).then_inc(ln3_ready, 1)

            def ln4(u):
                pool.wait_ge(ss4_ready, u + 1)
                cols = slice(u % 2 * TPH, (u % 2 + 1) * TPH)
                rstd_of(var4, ss4[:, cols], 1.0 / P, rstd4, ln4_step, u + 1, cols).then_inc(ln4_ready, 1)

            ln1(0)
            constants()
            more_constants()
            for b in range(B + 1):
                attn, ffn, more = b < B, b >= 1, b < B - 1
                u0, u1 = 2 * b - 2, 2 * b - 1
                if attn:
                    products(b, (1,))
                if ffn:
                    ln2(u1)
                if more:
                    ln1(b + 1)
                if attn:
                    products(b, (2,))
                if ffn and attn:
                    ln3(u1)
                if attn:
                    conv_start(b)
                    conv_taps(b, (1, 2, 3, 4))
                if ffn and attn:
                    ln4(u0)
                if attn:
                    conv_taps(b, (5, 6))
                    conv_chain.done()
                    ln2(2 * b)
                    ln3(2 * b)
                if ffn and more:
                    ln4(u1)
                if not attn:
                    ln3(u1)
                    ln4(u0 - 1)
                    ln4(u0)
                    ln4(u1)

        @block.scalar
        def _(act):
            def copy(dst, src):
                return nc.scalar.activation(dst, src, ACT.Copy)

            def evacuate(b, use, half, dst):
                act.wait_ge(psA_full, filled(b, use, half))
                copy(dst, psA[:, half, :]).then_inc(psA_free, 1)

            def normalise1(b):
                act.wait_ge(ln1_ready, upto(b, 1, 1))
                if b:
                    act.wait_ge(xn_kept, upto(b - 1, 1, 1))
                for j in range(NT):
                    nc.scalar.activation(xn[:, j, :], x_in[:, j, :], ACT.Identity, bias=nmr1[:, j:j + 1],
                                         scale=rstd1[:, j:j + 1]).then_inc(xn_ready, 1)

            def keep_normed(b):
                act.wait_ge(yc_ready, upto(b, 2, 0))
                copy(xn_res[:], xn[:]).then_inc(xn_kept, 1)

            def evacuate_x(b):
                for half in range(2):
                    evacuate(b - 1, PSA_X, half, xnT[:, bass.ts(half, HALF)])

            def evacuate_k(b):
                for half in range(2):
                    evacuate(b - 1, PSA_K, half, kT[:, PRE + half * HALF:PRE + (half + 1) * HALF])

            def evacuate_q(b):
                for half in range(2):
                    evacuate(b - 1, PSA_Q, half, qT[:, bass.ts(half, HALF)])

            def evacuate_v(b):
                act.wait_ge(conv_step, upto(b, N_CONV_STEPS, 0))
                for half in range(2):
                    evacuate(b - 1, PSA_V, half, vT[:, VPRE + half * HALF:VPRE + (half + 1) * HALF])

            def features(b):
                act.wait_ge(psA_free, freed(b - 1, PSA_Q, 1))
                nc.scalar.activation(kexp[:], kT[:, PRE:PRE + T], ACT.Exp)
                nc.scalar.activation(fkT[:], kT[:, PRE:PRE + T], ACT.Relu).then_inc(k_feat, 1)
                nc.scalar.activation(qexp[:], qT[:], ACT.Exp)
                act.wait_ge(low_used, b)
                nc.scalar.activation(fqT[:], qT[:], ACT.Relu).then_inc(q_feat, 1)

            def token_major_v(b):
                act.wait_ge(terms_ready, upto(b, NT, 0))
                for half in range(2):
                    evacuate(b, PSA_V_TOK, half, v_tok[:, half * TPH:(half + 1) * TPH, :].rearrange("p j c -> p (j c)"))

            def token_major_fk(b):
                for half in range(2):
                    evacuate(b, PSA_FK_TOK, half, fk_tok[:, half * TPH:(half + 1) * TPH, :].rearrange("p j c -> p (j c)"))

            def scores(b):
                for half in range(2):
                    evacuate(b, PSA_SCORES, half, scoresT[:, bass.ts(half, HALF)])

            def exponentials(b):
                act.wait_ge(logit_ready, upto(b, 1, 1))
                nc.scalar.activation(prob[:], logit[:], ACT.Exp, scale=float(HD) ** -0.5).then_inc(prob_ready, 1)

            def unit_tiles(u):
                return range(u % 2 * TPH, (u % 2 + 1) * TPH)

            def half_cols(u):
                return bass.ts(u % 2, HALF)

            def norm2(u):
                act.wait_ge(yc_ready, u + 1)
                for j in unit_tiles(u):
                    last = nc.scalar.activation(squares[:, j, :], yc[:, j, :], ACT.Square, accum_out=ss2[:, j:j + 1])
                last.then_inc(ss2_ready, 1)

            def norm3_squares(u):
                for n, j in enumerate(unit_tiles(u)):
                    act.wait_ge(x2_ready, upto(u, TPH, n + 1))
                    last = nc.scalar.activation(squares[:, j, :], x2_of(u)[:, j, :], ACT.Square,
                                                bias=neg_mean[:, u // 2 % 3, j:j + 1], accum_out=ss3[:, j:j + 1])
                last.then_inc(ss3_ready, 1)

            def normalise3(u):
                act.wait_ge(ln3_ready, u + 1)
                for j in unit_tiles(u):
                    last = nc.scalar.activation(xn3[:, j, :], x2_of(u)[:, j, :], ACT.Identity, bias=nmr3[:, j:j + 1],
                                                scale=rstd3[:, j:j + 1])
                last.then_inc(xn3_ready, 1)

            def evacuate_x3(u):
                act.wait_ge(front_full, upto(u, N_FRONT, 1))
                copy(x3T[:, half_cols(u)], front(u, X3)).then_inc(front_free, 1)

            def gate_logits(u):
                act.wait_ge(front_full, upto(u, N_FRONT, 2))
                copy(gate_shared[:, half_cols(u)], front(u, C4)).then_inc(front_free, 1)
                act.wait_ge(front_full, upto(u, N_FRONT, 3))
                if u:
                    act.wait_ge(gate_step, upto(u - 1, N_GATE_STEPS, 1))
                nc.scalar.activation(gexp[:], front(u, LOGITS)[:, 0:TPH * EXPERTS].rearrange("p (j e) -> p j e", e=EXPERTS),
                                     ACT.Exp, scale=-1.0).then_inc(front_free, 1)

            def hidden(u, chunks):
                if u == 0:
                    act.wait_ge(ffn_ld, N_FFN_LD)
                for c in chunks:
                    act.wait_ge(hidden_full, upto(u, N_HIDDEN, c + 1))
                    nc.scalar.activation(hid[:, c, half_cols(u)], hidden_bank(u, c), ACT.Gelu,
                                         bias=b1c[:, c:c + 1]).then_inc(hidden_free, 1)

            def shared_hidden(u):
                nc.scalar.activation(hid[HID:P, 4, half_cols(u)], gate_shared[HID:P, half_cols(u)], ACT.Gelu,
                                     bias=bs1c[HID:P, :])

            def gates_expert_major(u):
                act.wait_ge(gates_turned, u + 1)
                parts = psG[0:24, 1, :].bitcast(BF16)[:, 0:HALF]
                copy(gT[:], parts).then_inc(gT_ready, 1)
                copy(hid[0:24, 4, half_cols(u)], parts).then_inc(gT_ready, 1)

            def norm4(u):
                act.wait_ge(experts_summed, u + 1)
                y = outputs(u)
                for n, j in enumerate(unit_tiles(u)):
                    last = nc.scalar.activation(squares4[:, j, :], y[:, bass.ts(n, P)], ACT.Square, accum_out=ss4[:, j:j + 1])
                last.then_inc(ss4_ready, 1)

            normalise1(0)
            evacuate_x(0)
            evacuate_k(0)
            evacuate_q(0)
            features(0)
            evacuate_v(0)
            for b in range(B + 1):
                attn, ffn, more = b < B, b >= 1, b < B - 1
                u0, u1 = 2 * b - 2, 2 * b - 1
                if attn:
                    token_major_v(b)
                if attn:
                    if ffn:
                        evacuate_x3(u0)
                    token_major_fk(b)
                    if ffn:
                        gate_logits(u0)
                    keep_normed(b)
                    if ffn:
                        norm3_squares(u1)
                        hidden(u0, range(0, 2))
                        normalise3(u1)
                    scores(b)
                    if ffn:
                        hidden(u0, range(2, 4))
                        shared_hidden(u0)
                        gates_expert_major(u0)
                        evacuate_x3(u1)
                    if b == 0:
                        normalise1(b + 1)
                    exponentials(b)
                    if ffn:
                        gate_logits(u1)
                    if more and b:
                        normalise1(b + 1)
                    if ffn:
                        hidden(u1, range(0, 2))
                        norm4(u0)
                    if more:
                        evacuate_x(b + 1)
                    if ffn:
                        hidden(u1, range(2, 4))
                        shared_hidden(u1)
                    if more:
                        evacuate_k(b + 1)
                        evacuate_q(b + 1)
                    if b == 0:
                        features(b + 1)
                    if ffn:
                        gates_expert_major(u1)
                    norm2(2 * b)
                    if not more:
                        norm3_squares(2 * b)
                        norm2(2 * b + 1)
                        normalise3(2 * b)
                    if more:
                        evacuate_v(b + 1)
                    if more and b:
                        features(b + 1)
                    if more:
                        norm3_squares(2 * b)
                        norm2(2 * b + 1)
                        normalise3(2 * b)
                        if ffn:
                            norm4(u1)
                else:
                    evacuate_x3(u0)
                    norm3_squares(u1)
                    gate_logits(u0)
                    normalise3(u1)
                    evacuate_x3(u1)
                    gate_logits(u1)
                    hidden(u0, range(0, 2))
                    norm4(u0 - 1)
                    hidden(u0, range(2, 4))
                    shared_hidden(u0)
                    gates_expert_major(u0)
                    hidden(u1, range(4))
                    shared_hidden(u1)
                    gates_expert_major(u1)
                    norm4(u0)
                    norm4(u1)

        @block.vector
        def _(dve):
            nc.vector.memset(w1[:, 4 * P:5 * P], 0.0).then_inc(w_zeroed, 1)
            nc.vector.memset(w2[:, 4, :], 0.0).then_inc(w_zeroed, 1)
            nc.vector.memset(hid[0:32, 4, :], 1.0)
            nc.vector.memset(hid[32:HID, 4, :], 0.0)
            nc.vector.memset(ksum_sel[:], 0.0).then_inc(zeros_set, 1)

            def stats(b):
                dve.wait_ge(x_in_ld, upto(b, N_DMA, 16))
                for j in range(NT):
                    last = nc.vector.bn_stats(bn[:, j, :], x_in[:, j, :])
                last.then_inc(bn_done, 1)
                dve.wait_ge(bn_done, upto(b, 1, 1))
                for j in range(NT):
                    last = nc.vector.bn_aggr(mv[:, j, :], bn[:, j, :])
                last.then_inc(stats1, 1)

            def centre_weights():
                dve.wait_ge(consts_ready, 1)
                nc.vector.tensor_copy(identb[:], ident[:])
                dve.wait_ge(wo_ld, 16)
                nc.vector.tensor_reduce(row_mean[:, 0:1], wo[:], AX_X, ALU.add)
                dve.wait_ge(ffn_ld, N_FFN_LD)
                nc.vector.tensor_reduce(row_mean[:, 1:1 + CH], w2[:], AX_X, ALU.add).then_inc(w_means, 1)
                dve.wait_ge(w_means, 1)
                nc.vector.tensor_scalar(row_mean[:], row_mean[:], 1.0 / P, None, ALU.mult).then_inc(w_means, 1)
                dve.wait_ge(w_means, 2)
                nc.vector.tensor_scalar(wo[:], wo[:], row_mean[:, 0:1], None, ALU.subtract)
                nc.vector.tensor_tensor(w2[:], w2[:], row_mean[:, 1:1 + CH].unsqueeze(2).to_broadcast([P, CH, P]),
                                        ALU.subtract).then_inc(w_centred, 1)

            def key_features(b):
                dve.wait_ge(k_feat, upto(b, 1, 1))
                nc.vector.scalar_tensor_tensor(out=fkT[:], in0=kexp[:], scalar=1.0, in1=fkT[:], op0=ALU.min,
                                               op1=ALU.add, accum_out=ksum[:]).then_inc(fk_ready, 1)

            def query_features(b):
                dve.wait_ge(q_feat, upto(b, 1, 1))
                nc.vector.scalar_tensor_tensor(out=fqT[:], in0=qexp[:], scalar=1.0, in1=fqT[:], op0=ALU.min,
                                               op1=ALU.add).then_inc(fq_ready, 1)

            def products(b, s):
                if s == 0:
                    dve.wait_ge(psA_free, freed(b - 1, PSA_Q, 1))
                if s == 2:
                    dve.wait_ge(group_summed, upto(b, 2, 1))
                for q in range(QUADS):
                    if TERMS[SLOTS * q + s] != LOW and (s, q) not in POOL_PRODUCTS:
                        product(nc.vector, s, q).then_inc(prod_ready, 1)

            def linear_state(b):
                dve.wait_ge(fk_ready, upto(b, 1, 1))
                nc.vector.tensor_scalar(ksum_sel[:, 16:16 + HEADS], head_sel[:], ksum[:], None, ALU.mult)
                dve.wait_ge(kv_summed, upto(b, 1, 1))
                nc.vector.tensor_tensor(kv[:], psY[:, 0:P], head_mask[:], ALU.mult).then_inc(kv_ready, 1)

            def softmax_logits(b):
                dve.wait_ge(psA_full, filled(b, PSA_SCORES_T, 1))
                softmax_chain.start(dve, b)
                pz = psA[:].rearrange("p a (j r) -> p (a j) r", r=P)
                z0 = 32 * (M_LOW // SLOTS) + HEADS * (M_LOW % SLOTS)
                nc.vector.tensor_scalar(zden[:], pz[:, :, z0:z0 + HEADS], 1e-6, None, ALU.add)
                for half in range(2):
                    ins = nc.vector.tensor_tensor(
                        logit[:, half * TPH:(half + 1) * TPH].rearrange("p j (q s) h -> p (j q) (s h)", s=SLOTS),
                        psA[:, half, :].rearrange("p (r c) -> p r c", c=32)[:, :, 0:SLOTS * HEADS],
                        mask[:, half * TPH:(half + 1) * TPH].rearrange("p j (q s) h -> p (j q) (s h)", s=SLOTS),
                        ALU.add)
                    ins.then_inc(scores_read, 1)
                dve.wait_ge(scores_read, upto(b, 2, 2))
                softmax_chain(nc.vector.tensor_reduce(top[:], logit[:].rearrange("p j m h -> p j h m"), AX_X, ALU.max))
                nc.vector.tensor_tensor(logit[:], logit[:], top[:].unsqueeze(2).to_broadcast([P, NT, NM, HEADS]),
                                        ALU.subtract).then_inc(logit_ready, 1)

            def softmax_weights(b):
                dve.wait_ge(prob_ready, upto(b, 1, 1))
                softmax_chain(nc.vector.tensor_reduce(den[:], prob[:].rearrange("p j m h -> p j h m"), AX_X, ALU.add))
                softmax_chain(nc.vector.reciprocal(rden[:], den[:]))
                softmax_chain(nc.vector.tensor_tensor(wgt[:], prob[:],
                                                      rden[:].unsqueeze(2).to_broadcast([P, NT, NM, HEADS]),
                                                      ALU.mult))
                softmax_chain(nc.vector.reciprocal(wgt[:, :, M_LOW, :], zden[:]))

            def weigh_low(b):
                dve.wait_ge(low_ready, upto(b, 1, 1))
                w = wgt[:, :, M_LOW, :].unsqueeze(3).to_broadcast([P, NT, HEADS, HD])
                ins = nc.vector.tensor_tensor(low_terms.rearrange("p j (h d) -> p j h d", d=HD),
                                              psG[:].rearrange("p a (j h d) -> p (a j) h d", h=HEADS, d=HD),
                                              w, ALU.mult)
                ins.then_inc(low_used, 1)

            def weigh(b, j):
                if j == 0:
                    dve.wait_ge(v_shifted, upto(b, N_SHIFT_DMA, N_SHIFT_DMA))
                if j >= TERM_BUFS:
                    dve.wait_ge(terms_summed, upto(b, NT, j - TERM_BUFS + 1))
                n = 1 + min(j // 2, 2)

                def term(m0, m1, src):
                    w = wgt[:, j, m0:m1, :].unsqueeze(3).to_broadcast([P, m1 - m0, HEADS, HD])
                    dst = terms[:, j % TERM_BUFS, m0:m1, :].rearrange("p m (h d) -> p m h d", d=HD)
                    return nc.vector.tensor_tensor(dst, src.rearrange("p m (h d) -> p m h d", d=HD), w, ALU.mult)

                if n > 1:
                    term(M_TILES + 3 - n, M_TILES + 3, v_tok[:, j - 2 * (n - 1):j + 1:2, :])
                else:
                    term(M_TILES + 2, M_TILES + 3, v_tok[:, j:j + 1, :])
                if j >= 1:
                    term(M_128, M_128 + 1, v_tok[:, j - 1:j, :])
                term(M_SHIFT, M_LOW, v_shift[:, :, j, :]).then_inc(terms_ready, 1)

            def add_conv(b, half):
                dve.wait_ge(terms_summed, upto(b, NT, TPH * (half + 1)))
                dve.wait_ge(conv_step, upto(b, N_CONV_STEPS, N_CONV_STEPS))
                cols = bass.ts(half, HALF)
                nc.vector.tensor_tensor(hT[:, cols], psH[:], convT[:, cols], ALU.add).then_inc(hT_ready, 1)

            def add_normed(b, half):
                dve.wait_ge(y_ready, upto(b, 2, half + 1))
                dve.wait_ge(xn_kept, upto(b, 1, 1))
                tiles = slice(half * TPH, (half + 1) * TPH)
                nc.vector.tensor_tensor(yc[:, tiles, :], psY[:].rearrange("p (j c) -> p j c", c=P),
                                        xn_res[:, tiles, :], ALU.add).then_inc(yc_ready, 1)

            def residual(u):
                b, half = u // 2, u % 2
                dve.wait_ge(x_res_ld, upto(b, N_DMA, 16))
                dve.wait_ge(ln2_ready, u + 1)
                if 0 < b < B - 1:
                    dve.wait_ge(out_ready, upto(u - 1, TPH, 0))
                for j in range(half * TPH, (half + 1) * TPH):
                    nc.vector.scalar_tensor_tensor(out=x2_of(u)[:, j, :], in0=yc[:, j, :], scalar=rstd2[:, j:j + 1],
                                                   in1=x_res[:, j, :], op0=ALU.mult, op1=ALU.add).then_inc(x2_ready, 1)

            def gates(u, steps):
                bc = [P, TPH, EXPERTS]
                den_, sig, score, eq, cand, one1, rest, one2, both, g = (t[:] for t in gtmp)
                m1, c1, m2, c2, msum, mrec = (t[:] for t in gmax)
                tt, ts, red = nc.vector.tensor_tensor, nc.vector.tensor_scalar, nc.vector.tensor_reduce
                rec, copy = nc.vector.reciprocal, nc.vector.tensor_copy

                def spread(t):
                    return t.unsqueeze(2).to_broadcast(bc)

                for n in steps:
                    if n == 0:
                        dve.wait_ge(front_free, upto(u, N_FRONT, 3))
                    if n or u:
                        dve.wait_ge(gate_step, upto(u, N_GATE_STEPS, n))
                    if n == 0:
                        ins = ts(den_, gexp[:], 1.0, None, ALU.add)
                    elif n == 1:
                        ins = rec(sig, den_)
                    elif n == 2:
                        ins = ts(score, sig, rscale[:], None, ALU.mult)
                    elif n == 3:
                        ins = red(m1, score, AX_X, ALU.max)
                    elif n == 4:
                        ins = tt(eq, score, spread(m1), ALU.is_equal)
                    elif n == 5:
                        ins = tt(cand, eq, first_pref[:], ALU.mult)
                    elif n == 6:
                        ins = red(c1, cand, AX_X, ALU.max)
                    elif n == 7:
                        ins = tt(one1, cand, spread(c1), ALU.is_equal)
                    elif n == 8:
                        ins = nc.vector.scalar_tensor_tensor(out=rest, in0=one1, scalar=-BIG, in1=score,
                                                             op0=ALU.mult, op1=ALU.add)
                    elif n == 9:
                        ins = red(m2, rest, AX_X, ALU.max)
                    elif n == 10:
                        ins = tt(eq, rest, spread(m2), ALU.is_equal)
                    elif n == 11:
                        ins = tt(cand, eq, first_pref[:], ALU.mult)
                    elif n == 12:
                        ins = red(c2, cand, AX_X, ALU.max)
                    elif n == 13:
                        ins = tt(one2, cand, spread(c2), ALU.is_equal)
                    elif n == 14:
                        ins = tt(both, one1, one2, ALU.add)
                    elif n == 15:
                        ins = tt(both, both, score, ALU.mult)
                    elif n == 16:
                        ins = tt(msum, m1, m2, ALU.add)
                    elif n == 17:
                        ins = rec(mrec, msum)
                    elif n == 18:
                        ins = tt(g, both, spread(mrec), ALU.mult)
                    elif n == 19:
                        if u:
                            dve.wait_ge(gates_turned, u)
                        ins = copy(gparts[:, :, 0, :], g)
                    elif n == 20:
                        ins = tt(rest, g, gparts[:, :, 0, :], ALU.subtract)
                    elif n == 21:
                        ins = copy(gparts[:, :, 1, :], rest)
                    elif n == 22:
                        ins = tt(cand, rest, gparts[:, :, 1, :], ALU.subtract)
                    else:
                        ins = copy(gparts[:, :, 2, :], cand)
                    ins.then_inc(gate_step, 1)

            def gate_hidden(u, chunks):
                cols = bass.ts(u % 2, HALF)
                for c in chunks:
                    dve.wait_ge(gate_spread, upto(u, 4, c + 1))
                    nc.vector.tensor_tensor(hid[:, c, cols], hid[:, c, cols], psG[:, c % 2, :],
                                            ALU.mult).then_inc(gated, 1)

            def finish(u):
                if u >= 2:
                    dve.wait_ge(out_stored[u % 2], upto(u // 2, N_DMA, 0))
                dve.wait_ge(ln4_ready, u + 1)
                for n in range(TPH):
                    j = u % 2 * TPH + n
                    y = outputs(u)[:, bass.ts(n, P)]
                    nc.vector.scalar_tensor_tensor(out=y_out[:, j, :], in0=y, scalar=rstd4[:, j:j + 1],
                                                   in1=x2_of(u)[:, j, :], op0=ALU.mult, op1=ALU.add).then_inc(out_ready, 1)

            stats(0)
            dve.wait_ge(consts_ready, 1)
            dve.wait_ge(zeros_set, 1)
            for b in range(B + 1):
                attn, ffn, more = b < B, b >= 1, b < B - 1
                u0, u1 = 2 * b - 2, 2 * b - 1
                if attn:
                    products(b, 0)
                    if b == 0:
                        key_features(0)
                    query_features(b)
                    if b >= 2:
                        finish(u0 - 1)
                    if more:
                        stats(b + 1)
                if b == 0:
                    centre_weights()
                if attn:
                    products(b, 1)
                if ffn:
                    residual(u1)
                if attn:
                    products(b, 2)
                    linear_state(b)
                    if b == 0:
                        dve.wait_ge(consts_ready, 2)
                    if ffn:
                        gates(u0, range(0, 24))
                    softmax_logits(b)
                    if ffn:
                        gate_hidden(u0, range(0, 4))
                    softmax_weights(b)
                    weigh_low(b)
                    for j in range(NT):
                        weigh(b, j)
                        if ffn:
                            if j <= 2:
                                gates(u1, range(8 * j, 8 * (j + 1)))
                            if j == 3:
                                finish(u0)
                            if j in (5, 6):
                                gate_hidden(u1, range(2 * (j - 5), 2 * (j - 4)))
                        if j == TPH:
                            add_conv(b, 0)
                        if j == TPH + 1:
                            add_normed(b, 0)
                    residual(2 * b)
                    add_conv(b, 1)
                    if more:
                        key_features(b + 1)
                    add_normed(b, 1)
                else:
                    gates(u0, range(0, 24))
                    gates(u1, range(0, 24))
                    gate_hidden(u0, range(0, 4))
                    finish(u0 - 1)
                    gate_hidden(u1, range(0, 4))
                    finish(u0)
                    finish(u1)

        @block.tensor
        def _(pe):
            def claim_psA(b, use, half):
                if use == PSA_X:
                    if b >= 0:
                        pe.wait_ge(scores_read, upto(b, 2, half + 1))
                elif use == PSA_V_TOK:
                    pe.wait_ge(psA_free, freed(b - 1, PSA_V, half))
                else:
                    pe.wait_ge(psA_free, freed(b, use - 1, half))

            def turn(b, use, src, later_half=None):
                for j in range(NT):
                    h, cols = bank(j)
                    if j == TPH and later_half:
                        pe.wait_ge(*later_half)
                    if j % TPH == 0:
                        claim_psA(b, use, h)
                    ins = pe.transpose(psA[:, h, cols], src(j), ident[:])
                    if j % TPH == TPH - 1:
                        ins.then_inc(psA_full, 1)

            def project(b, use, part):
                for half in range(2):
                    claim_psA(b, use, half)
                    pe.matmul(psA[:, half, :], wqkv[:, bass.ts(part, P)], xnT[:, bass.ts(half, HALF)],
                              start=True, stop=True).then_inc(psA_full, 1)

            def turn_x(b):
                pe.wait_ge(xn_ready, upto(b, NT, TPH if b == 0 else NT))
                turn(b - 1, PSA_X, lambda j: xn[:, j, :], later_half=(xn_ready, NT) if b == 0 else None)

            def project_k(b):
                project(b - 1, PSA_K, 1)

            def project_q(b):
                project(b - 1, PSA_Q, 0)

            def project_v(b):
                project(b - 1, PSA_V, 2)

            def token_major_v(b):
                turn(b, PSA_V_TOK, lambda j: vT[:, VPRE + j * P:VPRE + (j + 1) * P])

            def token_major_fk(b):
                pe.wait_ge(fk_ready, upto(b, 1, 1))
                turn(b, PSA_FK_TOK, lambda j: fkT[:, bass.ts(j, P)])

            def linear_state(b, first):
                if not first:
                    pe.wait_ge(yc_ready, upto(b, 2, 0))
                pe.wait_ge(psA_free, freed(b, PSA_FK_TOK, 1))
                for j in range(NT):
                    ins = pe.matmul(psY[:, 0:P], fk_tok[:, j, :], v_tok[:, j, :], start=(j == 0), stop=(j == NT - 1))
                ins.then_inc(kv_summed, 1)

            def sum_heads(b, s):
                pe.wait_ge(prod_ready, upto(b, N_PRODUCTS[2], N_PRODUCTS[s]))
                if s:
                    pe.wait_ge(pool_prod_ready, upto(b, len(POOL_PRODUCTS), s + 1))
                if s == 2:
                    pe.wait_ge(fq_ready, upto(b, 1, 1))
                    pe.wait_ge(kv_ready, upto(b, 1, 1))
                for half in range(2):
                    if s == 0:
                        claim_psA(b, PSA_SCORES, half)
                    cols = bass.ts(half, HALF)
                    for q in range(QUADS):
                        off = TERMS[SLOTS * q + s]
                        none = off == 512 and half == 0
                        if none:
                            continue
                        low = off == LOW
                        ins = pe.matmul(psA[32 * q:32 * q + 32, half, :], ksum_sel[:] if low else slot_sel[:, s, :],
                                        fqT[:, cols] if low else prods[:, QUADS * (s % 2) + q, cols],
                                        start=(s == 0), stop=(s == 2))
                    if s == 2:
                        ins.then_inc(psA_full, 1)
                if s < 2:
                    ins.then_inc(group_summed, 1)

            def turn_scores(b):
                turn(b, PSA_SCORES_T, lambda j: scoresT[:, bass.ts(j, P)])

            def low(b):
                if b:
                    pe.wait_ge(gated, upto(b, 8, -4))
                for j in range(NT):
                    h, cols = bank(j)
                    ins = pe.matmul(psG[:, h, cols], fqT[:, bass.ts(j, P)], kv[:], start=True, stop=True)
                ins.then_inc(low_ready, 1)

            def sum_terms(b, j):
                pe.wait_ge(terms_ready, upto(b, NT, j + 1))
                if j % TPH == 0 and (b or j):
                    pe.wait_ge(hT_ready, upto(b, 2, j // TPH))
                dst = psH[:, bass.ts(j % TPH, P)]
                pe.matmul(dst, low_terms[:, j, :], ident[:], is_transpose=True, start=True, stop=False)
                live = [m for m in range(NV) if TERMS[m] < P or TERMS[m] // P <= j]
                for m in live:
                    ins = pe.matmul(dst, terms[:, j % TERM_BUFS, m, :], ident[:], is_transpose=True,
                                    start=False, stop=(m == live[-1]))
                ins.then_inc(terms_summed, 1)

            def output(b, half):
                pe.wait_ge(hT_ready, upto(b, 2, half + 1))
                if half:
                    pe.wait_ge(yc_ready, upto(b, 2, 1))
                elif b:
                    pe.wait_ge(out_ready, upto(2 * b - 1, TPH, 0))
                for j in range(TPH * half, TPH * (half + 1)):
                    ins = pe.matmul(psY[:, bass.ts(j % TPH, P)], hT[:, bass.ts(j, P)], wo[:], start=True, stop=True)
                ins.then_inc(y_ready, 1)

            def unit_tiles(u):
                return range(u % 2 * TPH, (u % 2 + 1) * TPH)

            def half_cols(u):
                return bass.ts(u % 2, HALF)

            def turn_x3(u):
                if u == 2 * B - 2:
                    pe.wait_ge(hT_ready, 2 * B)
                elif u == 2 * B - 1:
                    pe.wait_ge(front_free, upto(u, N_FRONT, 0))
                elif u:
                    pe.wait_ge(hidden_free, upto(u, N_HIDDEN, -(u % 2)))
                pe.wait_ge(xn3_ready, u + 1)
                for n, j in enumerate(unit_tiles(u)):
                    ins = pe.transpose(front(u, X3)[:, bass.ts(n, P)], xn3[:, j, :], ident[:])
                ins.then_inc(front_full, 1)

            def gate_logits(u):
                if u == 2 * B - 2:
                    pe.wait_ge(yc_ready, 2 * B)
                elif u < 2 * B - 2 and u % 2:
                    pe.wait_ge(hidden_free, upto(u, N_HIDDEN, 0))
                elif u < 2 * B - 2 and u:
                    pe.wait_ge(out_ready, upto(u, TPH, 0))
                pe.wait_ge(front_free, upto(u, N_FRONT, 1))
                pe.matmul(front(u, C4), w1[:, 4 * P:5 * P], x3T[:, half_cols(u)], start=True, stop=True).then_inc(front_full, 1)

            def turn_logits(u):
                pe.wait_ge(front_free, upto(u, N_FRONT, 2))
                for n, j in enumerate(unit_tiles(u)):
                    ins = pe.transpose(front(u, LOGITS)[:, bass.ts(n, EXPERTS)], gate_shared[0:EXPERTS, bass.ts(j, P)],
                                       ident[0:EXPERTS, 0:EXPERTS])
                ins.then_inc(front_full, 1)

            def hidden(u, chunks):
                for c in chunks:
                    if c >= 2 or u >= 2 * B - 2:
                        pe.wait_ge(hidden_free, upto(u, N_HIDDEN, c - 1))
                    else:
                        pe.wait_ge(front_free, upto(u, N_FRONT, c + 2))
                    pe.matmul(hidden_bank(u, c), w1[:, bass.ts(c, P)], x3T[:, half_cols(u)],
                              start=True, stop=True).then_inc(hidden_full, 1)

            def gates_expert_major(u, low_of):
                pe.wait_ge(low_used, low_of + 1)
                if u:
                    pe.wait_ge(gated, upto(u, 4, 0))
                pe.wait_ge(gate_step, upto(u, N_GATE_STEPS, N_GATE_STEPS))
                dst = psG[0:24, 1, :].bitcast(BF16)
                for n in range(TPH):
                    ins = pe.transpose(dst[:, bass.ts(n, P)], gparts[:, n].rearrange("p a e -> p (a e)"), identb[:])
                ins.then_inc(gates_turned, 1)

            def spread_gates(u, chunks):
                for c in chunks:
                    if c < 2:
                        pe.wait_ge(gT_ready, upto(u, 2, c + 1))
                    else:
                        pe.wait_ge(gated, upto(u, 4, c - 1))
                    pe.matmul(psG[:, c % 2, :], gate_sel[:, c, :], gT[:], start=True, stop=True).then_inc(gate_spread, 1)

            def experts_out(u):
                if u >= 2 * B - 3:
                    pe.wait_ge(scores_read, 2 * B)
                    if u == 2 * B - 1:
                        pe.wait_ge(out_ready, upto(u - 1, TPH, 0))
                elif u % 2:
                    pe.wait_ge(hidden_free, upto(u, N_HIDDEN, 3))
                else:
                    pe.wait_ge(kv_ready, u // 2 + 2)
                    pe.wait_ge(yc_ready, u + 2)
                dst = outputs(u)
                pe.wait_ge(hidden_free, upto(u, N_HIDDEN, 4))
                pe.wait_ge(gT_ready, upto(u, 2, 2))
                pe.wait_ge(gated, upto(u, 4, 4))
                for n, j in enumerate(unit_tiles(u)):
                    for c in range(CH):
                        ins = pe.matmul(dst[:, bass.ts(n, P)], hid[:, c, bass.ts(j, P)], w2[:, c, :],
                                        start=(c == 0), stop=(c == CH - 1))
                ins.then_inc(experts_summed, 1)

            pe.wait_ge(ident_ready, 1)
            pe.wait_ge(wqkv_ld, 16)
            turn_x(0)
            project_k(0)
            project_q(0)
            project_v(0)
            for b in range(B + 1):
                attn, ffn, more = b < B, b >= 1, b < B - 1
                u0, u1 = 2 * b - 2, 2 * b - 1
                if attn:
                    token_major_v(b)
                    token_major_fk(b)
                    if ffn:
                        turn_x3(u0)
                    if b == 0:
                        pe.wait_ge(consts_ready, 1)
                    sum_heads(b, 0)
                    if ffn:
                        gate_logits(u0)
                        turn_logits(u0)
                    linear_state(b, b == 0)
                    if ffn:
                        hidden(u0, range(0, 2))
                    sum_heads(b, 1)
                    sum_heads(b, 2)
                    if ffn:
                        hidden(u0, range(2, 4))
                    turn_scores(b)
                    if ffn:
                        gates_expert_major(u0, b - 1)
                        turn_x3(u1)
                        spread_gates(u0, range(2))
                        gate_logits(u1)
                        spread_gates(u0, range(2, 4))
                    low(b)
                    if b == 0:
                        pe.wait_ge(w_centred, 1)
                        turn_x(b + 1)
                        project_k(b + 1)
                        project_q(b + 1)
                    if ffn:
                        turn_logits(u1)
                        hidden(u1, range(0, 2))
                        experts_out(u0)
                    for j in range(NT):
                        if ffn:
                            if j == 2:
                                hidden(u1, range(2, 4))
                            if j == 4:
                                gates_expert_major(u1, b)
                            if j in (5, 6):
                                spread_gates(u1, range(2 * (j - 5), 2 * (j - 4)))
                        if more:
                            if j == 1 and b:
                                turn_x(b + 1)
                            if j == 3 and b:
                                project_k(b + 1)
                            if j == 4 and b:
                                project_q(b + 1)
                            if j == 6:
                                project_v(b + 1)
                        sum_terms(b, j)
                        if j == TPH:
                            output(b, 0)
                    output(b, 1)
                    if ffn:
                        experts_out(u1)
                else:
                    turn_x3(u0)
                    gate_logits(u0)
                    turn_logits(u0)
                    hidden(u0, range(0, 2))
                    turn_x3(u1)
                    gate_logits(u1)
                    turn_logits(u1)
                    gates_expert_major(u0, b - 1)
                    hidden(u0, range(2, 4))
                    spread_gates(u0, range(0, 4))
                    hidden(u1, range(4))
                    gates_expert_major(u1, b - 1)
                    spread_gates(u1, range(0, 2))
                    experts_out(u0)
                    spread_gates(u1, range(2, 4))
                    experts_out(u1)


_INS = ['L0_attn_x', 'L0_attn_Wqkv', 'L0_attn_Wo', 'L0_attn_conv_w', 'L0_ffn_gate_W', 'L0_ffn_W1', 'L0_ffn_b1',
        'L0_ffn_W2', 'L0_ffn_b2', 'L0_ffn_Ws1', 'L0_ffn_bs1', 'L0_ffn_Ws2', 'L0_ffn_bs2', 'L0_ffn_route_scale']


def kernel(**inputs):
    import concourse.bacc as bacc
    from concourse.bass_utils import run_bass_kernel_spmd

    nc = bacc.Bacc("TRN2", target_bir_lowering=False, num_devices=1)
    arrays, args = {}, []
    for name in _INS:
        a = np.ascontiguousarray(inputs[name])
        if a.ndim == 0:
            a = a.reshape(1)
        arrays[name] = a
        args.append(nc.dram_tensor(name, a.shape, mybir.dt.from_np(a.dtype), kind="ExternalInput").ap())
    shape = inputs['L0_attn_x'].shape
    args.append(nc.dram_tensor("out", shape, F32, kind="ExternalOutput").ap())
    block_kernel(nc, *args)
    r = run_bass_kernel_spmd(nc, [arrays], core_ids=[0])
    return r.results[0]["out"]
```

```python
from contextlib import ExitStack

import numpy as np

import concourse.bass as bass
from concourse import mybir

F32 = mybir.dt.float32
BF16 = mybir.dt.bfloat16
ALU = mybir.AluOpType
ACT = mybir.ActivationFunctionType
AX_X = mybir.AxisListType.X

P = 128
HEADS = 8
HD = P // HEADS
TAPS = 7
EXPERTS = 8
HID = 64
T = 1024
NT = T // P
HALF = 512
TPH = HALF // P
EPS = 1e-5
BIG = 3.0e38
PRE = 512
VPRE = 64

LOW = -1
TERMS = [128, 512, 256, 0, 1, 2, 4, 8, 16, 32, 64, LOW]
NM = len(TERMS)
M_LOW = TERMS.index(LOW)
M_128 = TERMS.index(128)
M_TILES = TERMS.index(512)
M_SHIFT = TERMS.index(1)
SHIFTS = TERMS[M_SHIFT:M_LOW]
NV = M_LOW
SLOTS, QUADS = 3, 4
POOL_PRODUCTS = ((1, 0), (1, 1), (2, 0))
TERM_BUFS = 4
WARM_UP = 28
FILL_SUM = 12
FILL_FRONT = 5
CH = 5

N_DMA = 16
N_SHIFT_DMA = 16 * 2 * len(SHIFTS)
N_PSA_FULL, N_PSA_FREE = 16, 14
PSA_V_TOK, PSA_FK_TOK, PSA_SCORES, PSA_SCORES_T, PSA_X, PSA_K, PSA_Q, PSA_V = range(8)
PSA_AHEAD = 2 * 4
N_PRODUCTS = (4, 6, 8)
N_SOFTMAX_STEPS = 5
N_CONV_STEPS = 2 * TAPS - 1
N_FRONT = 3
N_HIDDEN = 4
X3, C4, LOGITS = range(N_FRONT)
N_GATE_STEPS = 24
LAST_BANKS = (0, 1, 2, 3, 0, 1, 2, 0)
LAST_GATE_STEPS = (12, 15, 18, 21)


def upto(b, per_batch, n):
    return b * per_batch + n


def filled(b, use, half):
    return upto(b, N_PSA_FULL, PSA_AHEAD + 2 * use + half + 1)


def psF_bank(u, use):
    return upto(u, N_FRONT + N_HIDDEN, use) % 2


def freed(b, use, half):
    return upto(b, N_PSA_FREE, PSA_AHEAD + 2 * (use - (use > PSA_SCORES_T)) + half + 1)


class Chain:

    def __init__(self, sem, per_batch):
        self.sem, self.per_batch = sem, per_batch

    def start(self, eng, b):
        self.eng, self.b, self.n = eng, b, 0

    def __call__(self, ins):
        self.n += 1
        ins.then_inc(self.sem, 1)
        self.eng.wait_ge(self.sem, upto(self.b, self.per_batch, self.n))

    def done(self):
        assert self.n == self.per_batch, (self.n, self.per_batch)


def block_kernel(nc, x, Wqkv, Wo, conv_w, gate_W, W1, b1, W2, b2, Ws1, bs1, Ws2, bs2, route_scale, out):
    B = x.shape[0]
    x_tok = x.rearrange("b (j p) c -> b p j c", p=P)
    out_tok = out.rearrange("b (j p) c -> b p j c", p=P)

    with ExitStack() as ctx:
        def sb(name, shape, dt=F32):
            return ctx.enter_context(nc.sbuf_tensor(name, shape, dt))

        def psum(name, shape, dt=F32):
            return ctx.enter_context(nc.psum_tensor(name, shape, dt))

        def sem(name):
            return ctx.enter_context(nc.semaphore(name))

        ctx.enter_context(nc.allow_non_contiguous_dma(reason="small bias vectors"))

        ident = sb("ident", [P, P])
        identb = sb("identb", [P, P], BF16)
        head_sel = sb("head_sel", [P, HEADS])
        head_mask = sb("head_mask", [P, P])
        slot_sel = sb("slot_sel", [P, SLOTS, 32])
        ksum_sel = sb("ksum_sel", [P, 32])
        mask = sb("mask", [P, NT, NM, HEADS])
        first_pref = sb("first_pref", [P, TPH, EXPERTS])
        gate_sel = sb("gate_sel", [24, 4, P], BF16)
        table_load = sb("table_load", [P, 1])
        neg_half = sb("neg_half", [P, NT])
        wqkv = sb("wqkv", [P, 3 * P])
        wo = sb("wo", [P, P])
        cw = sb("cw", [P, TAPS])
        w1 = sb("w1", [P, CH * P])
        w2 = sb("w2", [P, CH, P])
        b1c = sb("b1c", [P, 4])
        bs1c = sb("bs1c", [P, 1])
        rscale = sb("rscale", [P, 1])
        row_mean = sb("row_mean", [P, 1 + CH])

        x_in = sb("x_in", [P, NT, P])
        x_res = sb("x_res", [P, NT, P])
        xn = sb("xn", [P, NT, P])
        xn_res = sb("xn_res", [P, NT, P])
        yc = sb("yc", [P, NT, P])
        x2 = sb("x2", [P, NT, P])
        xn3 = sb("xn3", [P, NT, P])
        fk_tok = sb("fk_tok", [P, NT, P])
        v_tok = sb("v_tok", [P, NT, P])
        bn = sb("bn", [P, NT, 6])
        mv = sb("mv", [P, NT, 2])
        neg_mean = sb("neg_mean", [P, 3, NT])
        var1, rstd1, nmr1 = sb("var1", [P, NT]), sb("rstd1", [P, NT]), sb("nmr1", [P, NT])
        ss2, var2, rstd2 = sb("ss2", [P, NT]), sb("var2", [P, NT]), sb("rstd2", [P, NT])
        ss3, var3, rstd3, nmr3 = sb("ss3", [P, NT]), sb("var3", [P, NT]), sb("rstd3", [P, NT]), sb("nmr3", [P, NT])
        ss4, var4, rstd4 = sb("ss4", [P, NT]), sb("var4", [P, NT]), sb("rstd4", [P, NT])
        squares, squares4 = sb("squares", [P, NT, P]), sb("squares4", [P, NT, P])
        logit = sb("logit", [P, NT, NM, HEADS])
        top = sb("top", [P, NT, HEADS])
        prob = sb("prob", [P, NT, NM, HEADS])
        den = sb("den", [P, NT, HEADS])
        rden = sb("rden", [P, NT, HEADS])
        zden = sb("zden", [P, NT, HEADS])
        wgt = sb("wgt", [P, NT, NM, HEADS])
        v_shift = sb("v_shift", [P, len(SHIFTS), NT, P])

        xnT = sb("xnT", [P, T])
        kT = sb("kT", [P, PRE + T])
        vT = sb("vT", [P, VPRE + T])
        qT = sb("qT", [P, T])
        kexp, fkT = sb("kexp", [P, T]), sb("fkT", [P, T])
        qexp, fqT = sb("qexp", [P, T]), sb("fqT", [P, T])
        ksum = sb("ksum", [P, 1])
        kv = sb("kv", [P, P])
        prods = sb("prods", [P, 2 * QUADS, T])
        convT = sb("convT", [P, T])
        tapT = sb("tapT", [P, T])
        space = prods[:].rearrange("p a t -> p (a t)")
        n_terms = TERM_BUFS * NV * P
        terms = space[:, 0:n_terms].rearrange("p (a m c) -> p a m c", a=TERM_BUFS, m=NV)
        low_terms = space[:, n_terms:n_terms + T].rearrange("p (j c) -> p j c", c=P)
        hT = space[:, n_terms + T:n_terms + 2 * T]
        scoresT = space[:, 7 * T:8 * T]
        assert n_terms + 2 * T <= 8 * T

        x3T = sb("x3T", [P, T])
        gate_shared = sb("gate_shared", [P, T])
        gexp = sb("gexp", [P, TPH, EXPERTS])
        gtmp = [sb(f"gtmp{i}", [P, TPH, EXPERTS]) for i in range(10)]
        gmax = [sb(f"gmax{i}", [P, TPH]) for i in range(6)]
        gparts = sb("gparts", [P, TPH, 3, EXPERTS], BF16)
        gT = sb("gT", [24, 2, HALF], BF16)
        hid = sb("hid", [P, CH, T])
        y_out = sb("y_out", [P, NT, P])

        psA = psum("psA", [P, 2, HALF])
        psG = psum("psG", [P, 2, HALF])
        psH = psum("psH", [P, HALF])
        psY = psum("psY", [P, HALF])
        psF = psum("psF", [P, 2, HALF])

        wqkv_ld, conv_ld, wo_ld, ffn_ld = sem("wqkv_ld"), sem("conv_ld"), sem("wo_ld"), sem("ffn_ld")
        x_in_ld, x_res_ld, out_stored = sem("x_in_ld"), sem("x_res_ld"), [sem(f"out_stored{h}") for h in range(2)]
        pool_set, zeros_set, consts_ready = sem("pool_set"), sem("zeros_set"), sem("consts_ready")
        ident_ready = sem("ident_ready")
        w_zeroed, w_means, w_centred = sem("w_zeroed"), sem("w_means"), sem("w_centred")
        stats1 = sem("stats1")
        bn_done = sem("bn_done")
        ln1_ready, ln2_ready, ln3_ready, ln4_ready = sem("ln1_ready"), sem("ln2_ready"), sem("ln3_ready"), sem("ln4_ready")
        ln1_step, ln2_step, ln3_step, ln4_step = sem("ln1_step"), sem("ln2_step"), sem("ln3_step"), sem("ln4_step")
        xn_ready, xn_kept = sem("xn_ready"), sem("xn_kept")
        psA_full, psA_free, scores_read = sem("psA_full"), sem("psA_free"), sem("scores_read")
        k_feat, q_feat = sem("k_feat"), sem("q_feat")
        fk_ready, fq_ready = sem("fk_ready"), sem("fq_ready")
        kv_summed, kv_ready = sem("kv_summed"), sem("kv_ready")
        prod_ready, group_summed = sem("prod_ready"), sem("group_summed")
        logit_ready, prob_ready, softmax_step = sem("logit_ready"), sem("prob_ready"), sem("softmax_step")
        v_shifted, low_ready, low_used = sem("v_shifted"), sem("low_ready"), sem("low_used")
        pool_prod_ready = sem("pool_prod_ready")
        terms_ready, terms_summed = sem("terms_ready"), sem("terms_summed")
        conv_step, hT_ready, y_ready, yc_ready = sem("conv_step"), sem("hT_ready"), sem("y_ready"), sem("yc_ready")
        ss2_ready, x2_ready, ss3_ready, xn3_ready = sem("ss2_ready"), sem("x2_ready"), sem("ss3_ready"), sem("xn3_ready")
        front_full, front_free = sem("front_full"), sem("front_free")
        hidden_full, hidden_free = sem("hidden_full"), sem("hidden_free")
        gates_turned, shared_ready = sem("gates_turned"), sem("shared_ready")
        gate_spread, gated = sem("gate_spread"), sem("gated")
        gate_step, gT_ready, experts_summed = sem("gate_step"), sem("gT_ready"), sem("experts_summed")
        ss4_ready, out_scaled = sem("ss4_ready"), sem("out_scaled")
        out_ready = [sem(f"out_ready{h}") for h in range(2)]

        softmax_chain = Chain(softmax_step, N_SOFTMAX_STEPS)
        conv_chain = Chain(conv_step, N_CONV_STEPS)

        def bank(tile):
            return tile // TPH, bass.ts(tile % TPH, P)

        def product(eng, s, q):
            off = TERMS[SLOTS * q + s]
            t0 = HALF if off == 512 else 0
            return eng.tensor_tensor(prods[:, QUADS * (s % 2) + q, t0:T], qT[:, t0:T],
                                     kT[:, PRE - off + t0:PRE - off + T], ALU.mult)

        def x2_of(u):
            return x2[:] if u < 2 * B - 2 else qexp[:].rearrange("p (j c) -> p j c", c=P)

        def front(u, use):
            if u < 2 * B - 2:
                return psF[:, psF_bank(u, use), :]
            return psY[:] if use == C4 else psH[:]

        def last_chunk(u, c):
            return N_HIDDEN * (u - (2 * B - 2)) + c

        def hidden_bank(u, c):
            if u < 2 * B - 2:
                return psF[:, psF_bank(u, N_FRONT + c), :]
            return (psF[:, 0, :], psF[:, 1, :], psY[:], psA[:, 0, :])[LAST_BANKS[last_chunk(u, c)]]

        def outputs(u):
            if u < 2 * B - 3:
                return psG[:, 0, :] if u % 2 else psY[:]
            return psY[:] if u == 2 * B - 1 else psA[:, u % 2, :]

        def output_tile(u, n):
            return (psH if u == 2 * B - 1 and n >= TPH // 2 else outputs(u))[:, bass.ts(n, P)]

        def end_parts(u):
            return [range(0, TPH // 2), range(TPH // 2, TPH)] if u == 2 * B - 1 else [range(TPH)]

        def turned_gates(u):
            return (psG[0:24, 1, :] if u < 2 * B - 1 else psH[0:24, :]).bitcast(BF16)[:, 0:HALF]

        block = ctx.enter_context(nc.Block())

        @block.sync
        def _(sp):
            sp.dma_start(x_in[:], x_tok[0]).then_inc(x_in_ld, 16)
            sp.dma_start(wqkv[:], Wqkv).then_inc(wqkv_ld, 16)
            sp.dma_start(cw[:], conv_w).then_inc(conv_ld, 16)
            sp.dma_start(wo[:], Wo).then_inc(wo_ld, 16)
            sp.dma_start(x_res[:], x_tok[0]).then_inc(x_res_ld, 16)
            sp.wait_ge(w_zeroed, 2)
            sp.dma_start(w1[:, 0:EXPERTS * HID].rearrange("d (e h) -> d e h", e=EXPERTS),
                         W1.rearrange("e d h -> d e h")).then_inc(ffn_ld, 16)
            sp.dma_start(w1[:, 4 * P:4 * P + EXPERTS], gate_W).then_inc(ffn_ld, 16)
            sp.dma_start(w1[:, 4 * P + HID:5 * P], Ws1).then_inc(ffn_ld, 16)
            sp.dma_start(w2[:, 0:4, :], W2.rearrange("(c e) h n -> (e h) c n", e=2)).then_inc(ffn_ld, 16)
            for part in range(3):
                sp.dma_start(w2[8 * part:8 * part + 8, 4, :], b2).then_inc(ffn_ld, 16)
            sp.dma_start(w2[24:25, 4, :], bs2.rearrange("(a n) -> a n", a=1)).then_inc(ffn_ld, 16)
            sp.dma_start(w2[HID:P, 4, :], Ws2).then_inc(ffn_ld, 16)
            sp.dma_start(b1c[:], b1.rearrange("(c e) h -> (e h) c", e=2)).then_inc(ffn_ld, 16)
            sp.dma_start(bs1c[HID:P, :], bs1.rearrange("(h a) -> h a", a=1)).then_inc(ffn_ld, 16)
            sp.dma_start(rscale[:], route_scale.rearrange("(a n) -> a n", a=1).to_broadcast([P, 1])).then_inc(ffn_ld, 16)

            def load_next(b):
                sp.wait_ge(xn_ready, upto(b, NT, NT))
                sp.dma_start(x_in[:], x_tok[b + 1]).then_inc(x_in_ld, 16)

            def load_residual(b):
                sp.wait_ge(x2_ready, upto(b, NT, 0))
                sp.dma_start(x_res[:], x_tok[b]).then_inc(x_res_ld, 16)

            def shift_v(b):
                sp.wait_ge(psA_free, freed(b, PSA_V_TOK, 1))
                for n, off in enumerate(SHIFTS):
                    sp.dma_start(v_shift[off:P, n], v_tok[0:P - off]).then_inc(v_shifted, 16)
                    sp.dma_start(v_shift[0:off, n, 1:NT], v_tok[P - off:P, 0:NT - 1]).then_inc(v_shifted, 16)

            def store(u):
                for part in end_parts(u):
                    sp.wait_ge(out_ready[u % 2], upto(u // 2, TPH, part[-1] + 1))
                    tiles = slice(u % 2 * TPH + part[0], u % 2 * TPH + part[-1] + 1)
                    sp.dma_start(out_tok[u // 2][:, tiles], y_out[:, tiles]).then_inc(out_stored[u % 2], 16)

            for b in range(B + 1):
                if b < B - 1:
                    load_next(b)
                if b < B:
                    shift_v(b)
                if b >= 2:
                    store(2 * b - 3)
                if 1 <= b < B:
                    load_residual(b)
                if b:
                    store(2 * b - 2)
            store(2 * B - 1)
            for half in range(2):
                sp.wait_ge(out_stored[half], upto(B, N_DMA, half * N_DMA))

        N_FFN_LD = 16 * 12

        @block.gpsimd
        def _(pool):
            nc.gpsimd.memset(neg_half[:], -0.5)
            nc.gpsimd.memset(ident[:], 0.0)
            nc.gpsimd.memset(head_sel[:], 1.0)
            nc.gpsimd.memset(head_mask[:], 1.0)
            nc.gpsimd.memset(slot_sel[:], 0.0)
            nc.gpsimd.memset(gate_sel[:], 0.0)
            nc.gpsimd.memset(mask[:], 0.0).then_inc(pool_set, 1)
            pool.wait_ge(pool_set, 1)
            nc.gpsimd.affine_select(out=ident[:], in_=ident[:], compare_op=ALU.not_equal, fill=1.0, base=0,
                                    pattern=[[-1, P]], channel_multiplier=1).then_inc(ident_ready, 1)

            def constants():
                nc.gpsimd.affine_select(out=head_sel[:], in_=head_sel[:], compare_op=ALU.is_ge, fill=0.0, base=0,
                                        pattern=[[-HD, HEADS]], channel_multiplier=1)
                v = head_mask[:].rearrange("p (h d) -> p h d", h=HEADS)
                nc.gpsimd.affine_select(out=v, in_=v, compare_op=ALU.is_ge, fill=0.0, base=0,
                                        pattern=[[-HD, HEADS], [0, HD]], channel_multiplier=1).then_inc(pool_set, 1)
                pool.wait_ge(pool_set, 2)
                nc.gpsimd.affine_select(out=head_sel[:], in_=head_sel[:], compare_op=ALU.is_ge, fill=0.0, base=HD - 1,
                                        pattern=[[HD, HEADS]], channel_multiplier=-1)
                nc.gpsimd.affine_select(out=v, in_=v, compare_op=ALU.is_ge, fill=0.0, base=HD - 1,
                                        pattern=[[HD, HEADS], [0, HD]], channel_multiplier=-1).then_inc(pool_set, 1)
                pool.wait_ge(pool_set, 3)
                for s in range(SLOTS):
                    nc.gpsimd.tensor_copy(slot_sel[:, s, HEADS * s:HEADS * s + HEADS], head_sel[:])
                nc.gpsimd.memset(kT[:, 0:PRE], 0.0)
                nc.gpsimd.memset(vT[:, 0:VPRE], 0.0).then_inc(consts_ready, 1)

            def more_constants():
                for m, off in enumerate(TERMS):
                    v = mask[:, :, m, :]
                    if off == LOW:
                        nc.gpsimd.memset(v, -BIG)
                    else:
                        nc.gpsimd.affine_select(out=v, in_=v, compare_op=ALU.is_ge, fill=-BIG, base=-off,
                                                pattern=[[P, NT], [0, HEADS]], channel_multiplier=1)
                for n, off in enumerate(SHIFTS):
                    nc.gpsimd.memset(v_shift[0:off, n, 0, :], 0.0)
                for e in range(EXPERTS):
                    nc.gpsimd.memset(first_pref[:, :, e:e + 1], float(EXPERTS - e))
                for part in range(3):
                    v = gate_sel[:].rearrange("r c (a n) -> r c a n", a=2)
                    nc.gpsimd.affine_select(out=v, in_=v, compare_op=ALU.not_equal, fill=1.0, base=-EXPERTS * part,
                                            pattern=[[-2, 4], [-1, 2], [0, HID]],
                                            channel_multiplier=1).then_inc(pool_set, 1)
                    pool.wait_ge(pool_set, 4 + part)
                nc.gpsimd.memset(neg_half[0:1, 0:1], -0.5).then_inc(consts_ready, 1)

            def rstd_of(var, src, scale, rstd, step, value, cols):
                nc.gpsimd.tensor_scalar(var[:, cols], src, scale, EPS, ALU.mult, ALU.add).then_inc(step, 1)
                pool.wait_ge(step, value)
                return nc.gpsimd.tensor_tensor(rstd[:, cols], var[:, cols], neg_half[:, cols], ALU.pow)

            def ln1(b):
                pool.wait_ge(stats1, upto(b, 1, 1))
                if b >= 3:
                    pool.wait_ge(ln3_ready, 2 * (b - 2))
                nc.gpsimd.tensor_scalar(neg_mean[:, b % 3, :], mv[:, :, 0], -1.0, 0.0, ALU.mult, ALU.add)
                rstd_of(var1, mv[:, :, 1], 1.0, rstd1, ln1_step, upto(b, 2, 1), slice(0, NT)).then_inc(ln1_step, 1)
                pool.wait_ge(ln1_step, upto(b, 2, 2))
                nc.gpsimd.tensor_tensor(nmr1[:], neg_mean[:, b % 3, :], rstd1[:], ALU.mult).then_inc(ln1_ready, 1)

            def products(b, slots):
                for s in slots:
                    if s == 1:
                        pool.wait_ge(psA_free, freed(b - 1, PSA_Q, 1))
                        pool.wait_ge(y_ready, upto(b, 2, 0))
                    else:
                        pool.wait_ge(group_summed, upto(b, 2, 1))
                    for q in range(QUADS):
                        if (s, q) in POOL_PRODUCTS:
                            product(nc.gpsimd, s, q).then_inc(pool_prod_ready, 1)

            def conv_start(b):
                pool.wait_ge(psA_free, freed(b - 1, PSA_V, 1))
                if b == 0:
                    pool.wait_ge(conv_ld, 16)
                else:
                    pool.wait_ge(hT_ready, upto(b, 2, 0))
                conv_chain.start(pool, b)
                conv_chain(nc.gpsimd.tensor_scalar(convT[:], vT[:, VPRE:VPRE + T], cw[:, TAPS - 1:TAPS], 0.0,
                                                   ALU.mult, ALU.add))

            def conv_taps(b, shifts):
                for shift in shifts:
                    conv_chain(nc.gpsimd.tensor_scalar(tapT[:], vT[:, VPRE - shift:VPRE - shift + T],
                                                       cw[:, TAPS - 1 - shift:TAPS - shift], 0.0,
                                                       ALU.mult, ALU.add))
                    conv_chain(nc.gpsimd.tensor_tensor(convT[:], convT[:], tapT[:], ALU.add))

            def ln2(u):
                pool.wait_ge(ss2_ready, u + 1)
                cols = slice(u % 2 * TPH, (u % 2 + 1) * TPH)
                rstd_of(var2, ss2[:, cols], 1.0 / P, rstd2, ln2_step, u + 1, cols).then_inc(ln2_ready, 1)

            def ln3(u):
                pool.wait_ge(ss3_ready, u + 1)
                cols = slice(u % 2 * TPH, (u % 2 + 1) * TPH)
                rstd_of(var3, ss3[:, cols], 1.0 / P, rstd3, ln3_step, upto(u, 2, 1), cols).then_inc(ln3_step, 1)
                pool.wait_ge(ln3_step, upto(u, 2, 2))
                nc.gpsimd.tensor_tensor(nmr3[:, cols], neg_mean[:, u // 2 % 3, cols], rstd3[:, cols],
                                        ALU.mult).then_inc(ln3_ready, 1)

            def ln4(u):
                if u == 2 * B - 1:
                    pool.wait_ge(out_ready[1], upto(B - 1, TPH, 0))
                for i, part in enumerate(end_parts(u)):
                    pool.wait_ge(ss4_ready, u + 1 + i)
                    cols = slice(u % 2 * TPH + part[0], u % 2 * TPH + part[-1] + 1)
                    rstd_of(var4, ss4[:, cols], 1.0 / P, rstd4, ln4_step, u + 1 + i, cols).then_inc(ln4_ready, 1)

            def add_residual(u):
                tiles = slice(0, TPH)
                pool.wait_ge(out_scaled, u // 2 + 1)
                nc.gpsimd.tensor_tensor(y_out[:, tiles, :], y_out[:, tiles, :], x2[:, tiles, :],
                                        ALU.add).then_inc(out_ready[0], TPH)

            ln1(0)
            constants()
            more_constants()
            products(0, (1,))
            for b in range(B + 1):
                attn, ffn, more = b < B, b >= 1, b < B - 1
                u0, u1 = 2 * b - 2, 2 * b - 1
                if ffn:
                    ln2(u1)
                if 2 <= b < B:
                    ln4(u0 - 1)
                if attn:
                    products(b, (2,))
                if more:
                    ln1(b + 1)
                if ffn and attn:
                    ln3(u1)
                if attn:
                    conv_start(b)
                    conv_taps(b, range(1, TAPS))
                    conv_chain.done()
                if ffn and attn:
                    ln4(u0)
                    add_residual(u0)
                if attn:
                    ln2(2 * b)
                if more:
                    products(b + 1, (1,))
                if attn:
                    ln3(2 * b)
                if not attn:
                    ln3(u1)
                    ln4(u0 - 1)
                    ln4(u0)
                    ln4(u1)

        @block.scalar
        def _(act):
            def copy(dst, src):
                return nc.scalar.activation(dst, src, ACT.Copy)

            def evacuate(b, use, half, dst):
                act.wait_ge(psA_full, filled(b, use, half))
                copy(dst, psA[:, half, :]).then_inc(psA_free, 1)

            def normalise1(b, tiles=range(NT)):
                act.wait_ge(ln1_ready, upto(b, 1, 1))
                if b:
                    act.wait_ge(xn_kept, upto(b - 1, 1, 1))
                for j in tiles:
                    nc.scalar.activation(xn[:, j, :], x_in[:, j, :], ACT.Identity, bias=nmr1[:, j:j + 1],
                                         scale=rstd1[:, j:j + 1]).then_inc(xn_ready, 1)

            def keep_normed(b):
                act.wait_ge(yc_ready, upto(b, 2, 0))
                copy(xn_res[:], xn[:]).then_inc(xn_kept, 1)

            def evacuate_x(b):
                for half in range(2):
                    evacuate(b - 1, PSA_X, half, xnT[:, bass.ts(half, HALF)])

            def evacuate_k(b):
                for half in range(2):
                    evacuate(b - 1, PSA_K, half, kT[:, PRE + half * HALF:PRE + (half + 1) * HALF])

            def evacuate_q(b):
                for half in range(2):
                    evacuate(b - 1, PSA_Q, half, qT[:, bass.ts(half, HALF)])

            def evacuate_v(b):
                act.wait_ge(conv_step, upto(b, N_CONV_STEPS, 0))
                for half in range(2):
                    evacuate(b - 1, PSA_V, half, vT[:, VPRE + half * HALF:VPRE + (half + 1) * HALF])

            def features(b):
                act.wait_ge(psA_free, freed(b - 1, PSA_Q, 1))
                nc.scalar.activation(kexp[:], kT[:, PRE:PRE + T], ACT.Exp)
                nc.scalar.activation(fkT[:], kT[:, PRE:PRE + T], ACT.Relu).then_inc(k_feat, 1)
                nc.scalar.activation(qexp[:], qT[:], ACT.Exp)
                act.wait_ge(low_used, b)
                nc.scalar.activation(fqT[:], qT[:], ACT.Relu).then_inc(q_feat, 1)

            def token_major_v(b):
                act.wait_ge(terms_ready, upto(b, NT, 0))
                for half in range(2):
                    evacuate(b, PSA_V_TOK, half, v_tok[:, half * TPH:(half + 1) * TPH, :].rearrange("p j c -> p (j c)"))

            def token_major_fk(b):
                for half in range(2):
                    evacuate(b, PSA_FK_TOK, half, fk_tok[:, half * TPH:(half + 1) * TPH, :].rearrange("p j c -> p (j c)"))

            def scores(b):
                for half in range(2):
                    evacuate(b, PSA_SCORES, half, scoresT[:, bass.ts(half, HALF)])

            def exponentials(b):
                act.wait_ge(logit_ready, upto(b, 1, 1))
                nc.scalar.activation(prob[:], logit[:], ACT.Exp, scale=float(HD) ** -0.5).then_inc(prob_ready, 1)

            def unit_tiles(u):
                return range(u % 2 * TPH, (u % 2 + 1) * TPH)

            def half_cols(u):
                return bass.ts(u % 2, HALF)

            def norm2(u):
                act.wait_ge(yc_ready, u + 1)
                for j in unit_tiles(u):
                    last = nc.scalar.activation(squares[:, j, :], yc[:, j, :], ACT.Square, accum_out=ss2[:, j:j + 1])
                last.then_inc(ss2_ready, 1)

            def norm3_squares(u):
                for n, j in enumerate(unit_tiles(u)):
                    act.wait_ge(x2_ready, upto(u, TPH, n + 1))
                    last = nc.scalar.activation(squares[:, j, :], x2_of(u)[:, j, :], ACT.Square,
                                                bias=neg_mean[:, u // 2 % 3, j:j + 1], accum_out=ss3[:, j:j + 1])
                last.then_inc(ss3_ready, 1)

            def normalise3(u):
                act.wait_ge(ln3_ready, u + 1)
                for j in unit_tiles(u):
                    last = nc.scalar.activation(xn3[:, j, :], x2_of(u)[:, j, :], ACT.Identity, bias=nmr3[:, j:j + 1],
                                                scale=rstd3[:, j:j + 1])
                last.then_inc(xn3_ready, 1)

            def evacuate_x3(u):
                act.wait_ge(front_full, upto(u, N_FRONT, 1))
                copy(x3T[:, half_cols(u)], front(u, X3)).then_inc(front_free, 1)

            def gate_logits(u):
                act.wait_ge(front_full, upto(u, N_FRONT, 2))
                copy(gate_shared[:, half_cols(u)], front(u, C4)).then_inc(front_free, 1)
                act.wait_ge(front_full, upto(u, N_FRONT, 3))
                if u:
                    act.wait_ge(gate_step, upto(u - 1, N_GATE_STEPS, 1))
                nc.scalar.activation(gexp[:], front(u, LOGITS)[:, 0:TPH * EXPERTS].rearrange("p (j e) -> p j e", e=EXPERTS),
                                     ACT.Exp, scale=-1.0).then_inc(front_free, 1)

            def hidden(u, chunks):
                if u == 0:
                    act.wait_ge(ffn_ld, N_FFN_LD)
                for c in chunks:
                    act.wait_ge(hidden_full, upto(u, N_HIDDEN, c + 1))
                    nc.scalar.activation(hid[:, c, half_cols(u)], hidden_bank(u, c), ACT.Gelu,
                                         bias=b1c[:, c:c + 1]).then_inc(hidden_free, 1)

            def shared_hidden(u):
                nc.scalar.activation(hid[HID:P, 4, half_cols(u)], gate_shared[HID:P, half_cols(u)], ACT.Gelu,
                                     bias=bs1c[HID:P, :]).then_inc(shared_ready, 1)

            def gates_expert_major(u):
                act.wait_ge(gates_turned, u + 1)
                copy(gT[:, u % 2, :], turned_gates(u)).then_inc(gT_ready, 1)

            def gate_rows(u):
                act.wait_ge(gT_ready, u + 1)
                copy(hid[0:24, 4, half_cols(u)], gT[:, u % 2, :]).then_inc(shared_ready, 1)

            def norm4(u):
                if u == 2 * B - 1:
                    act.wait_ge(ln4_step, u - 1)
                for i, part in enumerate(end_parts(u)):
                    act.wait_ge(experts_summed, u + 1 + i)
                    for n in part:
                        j = unit_tiles(u)[n]
                        last = nc.scalar.activation(squares4[:, j, :], output_tile(u, n), ACT.Square,
                                                    accum_out=ss4[:, j:j + 1])
                    last.then_inc(ss4_ready, 1)

            def scale_outputs(u):
                if u >= 2:
                    act.wait_ge(out_stored[0], upto(u // 2, N_DMA, 0))
                act.wait_ge(ln4_ready, u + 1)
                for j in range(TPH):
                    last = nc.scalar.activation(y_out[:, j, :], outputs(u)[:, bass.ts(j, P)], ACT.Copy,
                                                scale=rstd4[:, j:j + 1])
                last.then_inc(out_scaled, 1)

            normalise1(0)
            evacuate_x(0)
            evacuate_k(0)
            evacuate_q(0)
            features(0)
            evacuate_v(0)
            for b in range(B + 1):
                attn, ffn, more = b < B, b >= 1, b < B - 1
                u0, u1 = 2 * b - 2, 2 * b - 1
                if attn:
                    if b == 0:
                        token_major_v(b)
                    if b == 0:
                        token_major_fk(b)
                    if ffn:
                        evacuate_x3(u0)
                    if ffn:
                        gate_logits(u0)
                    keep_normed(b)
                    if ffn:
                        norm3_squares(u1)
                        hidden(u0, range(0, 2))
                    if more and b:
                        normalise1(b + 1, range(0, TPH))
                    scores(b)
                    if more:
                        normalise1(b + 1, range(TPH if b else 0, NT))
                    if ffn:
                        normalise3(u1)
                        hidden(u0, range(2, 4))
                        shared_hidden(u0)
                        gates_expert_major(u0)
                        gate_rows(u0)
                        evacuate_x3(u1)
                    exponentials(b)
                    if ffn:
                        gate_logits(u1)
                    if more:
                        evacuate_x(b + 1)
                        evacuate_k(b + 1)
                    if ffn:
                        hidden(u1, range(0, 2))
                    if ffn:
                        norm4(u0)
                    if more:
                        evacuate_q(b + 1)
                    if ffn:
                        scale_outputs(u0)
                    if ffn:
                        hidden(u1, range(2, 4))
                        shared_hidden(u1)
                        gates_expert_major(u1)
                        gate_rows(u1)
                    if more:
                        features(b + 1)
                    norm2(2 * b)
                    if not more:
                        norm3_squares(2 * b)
                        nc.scalar.activation(table_load[:], neg_half[:, 0:1], ACT.Exp)
                        norm2(2 * b + 1)
                        normalise3(2 * b)
                    if more:
                        evacuate_v(b + 1)
                    if more:
                        token_major_v(b + 1)
                        token_major_fk(b + 1)
                        norm3_squares(2 * b)
                        norm2(2 * b + 1)
                        normalise3(2 * b)
                        if ffn:
                            norm4(u1)
                else:
                    evacuate_x3(u0)
                    norm3_squares(u1)
                    gate_logits(u0)
                    normalise3(u1)
                    evacuate_x3(u1)
                    gate_logits(u1)
                    shared_hidden(u0)
                    gates_expert_major(u0)
                    hidden(u0, range(0, 4))
                    gate_rows(u0)
                    hidden(u1, range(0, 4))
                    gates_expert_major(u1)
                    shared_hidden(u1)
                    gate_rows(u1)
                    norm4(u0 - 1)
                    norm4(u0)
                    norm4(u1)

        @block.vector
        def _(dve):
            nc.vector.memset(w1[:, 4 * P:5 * P], 0.0).then_inc(w_zeroed, 1)
            nc.vector.memset(w2[:, 4, :], 0.0).then_inc(w_zeroed, 1)
            nc.vector.memset(hid[0:32, 4, :], 1.0)
            nc.vector.memset(hid[32:HID, 4, :], 0.0)
            nc.vector.memset(ksum_sel[:], 0.0).then_inc(zeros_set, 1)

            def stats(b):
                dve.wait_ge(x_in_ld, upto(b, N_DMA, 16))
                for j in range(NT):
                    last = nc.vector.bn_stats(bn[:, j, :], x_in[:, j, :])
                last.then_inc(bn_done, 1)
                dve.wait_ge(bn_done, upto(b, 1, 1))
                for j in range(NT):
                    last = nc.vector.bn_aggr(mv[:, j, :], bn[:, j, :])
                last.then_inc(stats1, 1)

            def centre_weights():
                dve.wait_ge(consts_ready, 1)
                nc.vector.tensor_copy(identb[:], ident[:])
                dve.wait_ge(wo_ld, 16)
                nc.vector.tensor_reduce(row_mean[:, 0:1], wo[:], AX_X, ALU.add)
                dve.wait_ge(ffn_ld, N_FFN_LD)
                nc.vector.tensor_reduce(row_mean[:, 1:1 + CH], w2[:], AX_X, ALU.add).then_inc(w_means, 1)
                dve.wait_ge(w_means, 1)
                nc.vector.tensor_scalar(row_mean[:], row_mean[:], 1.0 / P, None, ALU.mult).then_inc(w_means, 1)
                dve.wait_ge(w_means, 2)
                nc.vector.tensor_scalar(wo[:], wo[:], row_mean[:, 0:1], None, ALU.subtract)
                nc.vector.tensor_tensor(w2[:], w2[:], row_mean[:, 1:1 + CH].unsqueeze(2).to_broadcast([P, CH, P]),
                                        ALU.subtract).then_inc(w_centred, 1)

            def key_features(b):
                dve.wait_ge(k_feat, upto(b, 1, 1))
                nc.vector.scalar_tensor_tensor(out=fkT[:], in0=kexp[:], scalar=1.0, in1=fkT[:], op0=ALU.min,
                                               op1=ALU.add, accum_out=ksum[:]).then_inc(fk_ready, 1)

            def query_features(b):
                dve.wait_ge(q_feat, upto(b, 1, 1))
                nc.vector.scalar_tensor_tensor(out=fqT[:], in0=qexp[:], scalar=1.0, in1=fqT[:], op0=ALU.min,
                                               op1=ALU.add).then_inc(fq_ready, 1)

            def products(b, s, beside=lambda n: None):
                if s == 0:
                    dve.wait_ge(psA_free, freed(b - 1, PSA_Q, 1))
                if s == 2:
                    dve.wait_ge(group_summed, upto(b, 2, 1))
                mine = [q for q in range(QUADS) if TERMS[SLOTS * q + s] != LOW and (s, q) not in POOL_PRODUCTS]
                for n, q in enumerate(mine):
                    product(nc.vector, s, q).then_inc(prod_ready, 1)
                    beside(n)

            def linear_state(b, beside):
                dve.wait_ge(fk_ready, upto(b, 1, 1))
                nc.vector.tensor_scalar(ksum_sel[:, 16:16 + HEADS], head_sel[:], ksum[:], None, ALU.mult)
                beside(0)
                dve.wait_ge(kv_summed, upto(b, 1, 1))
                nc.vector.tensor_tensor(kv[:], psY[:, 0:P], head_mask[:], ALU.mult).then_inc(kv_ready, 1)
                beside(1)

            def softmax_logits(b):
                dve.wait_ge(psA_full, filled(b, PSA_SCORES_T, 1))
                softmax_chain.start(dve, b)
                pz = psA[:].rearrange("p a (j r) -> p (a j) r", r=P)
                z0 = 32 * (M_LOW // SLOTS) + HEADS * (M_LOW % SLOTS)
                nc.vector.tensor_scalar(zden[:], pz[:, :, z0:z0 + HEADS], 1e-6, None, ALU.add)
                for half in range(2):
                    ins = nc.vector.tensor_tensor(
                        logit[:, half * TPH:(half + 1) * TPH].rearrange("p j (q s) h -> p (j q) (s h)", s=SLOTS),
                        psA[:, half, :].rearrange("p (r c) -> p r c", c=32)[:, :, 0:SLOTS * HEADS],
                        mask[:, half * TPH:(half + 1) * TPH].rearrange("p j (q s) h -> p (j q) (s h)", s=SLOTS),
                        ALU.add)
                    ins.then_inc(scores_read, 1)
                dve.wait_ge(scores_read, upto(b, 2, 2))
                softmax_chain(nc.vector.tensor_reduce(top[:], logit[:].rearrange("p j m h -> p j h m"), AX_X, ALU.max))
                nc.vector.tensor_tensor(logit[:], logit[:], top[:].unsqueeze(2).to_broadcast([P, NT, NM, HEADS]),
                                        ALU.subtract).then_inc(logit_ready, 1)

            def softmax_weights(b):
                dve.wait_ge(prob_ready, upto(b, 1, 1))
                softmax_chain(nc.vector.tensor_reduce(den[:], prob[:].rearrange("p j m h -> p j h m"), AX_X, ALU.add))
                softmax_chain(nc.vector.reciprocal(rden[:], den[:]))
                softmax_chain(nc.vector.tensor_tensor(wgt[:], prob[:],
                                                      rden[:].unsqueeze(2).to_broadcast([P, NT, NM, HEADS]),
                                                      ALU.mult))
                softmax_chain(nc.vector.reciprocal(wgt[:, :, M_LOW, :], zden[:]))

            def weigh_low(b):
                dve.wait_ge(low_ready, upto(b, 1, 1))
                for half, src in enumerate((psH, psY)):
                    tiles = slice(half * TPH, (half + 1) * TPH)
                    w = wgt[:, tiles, M_LOW, :].unsqueeze(3).to_broadcast([P, TPH, HEADS, HD])
                    ins = nc.vector.tensor_tensor(low_terms[:, tiles].rearrange("p j (h d) -> p j h d", d=HD),
                                                  src[:].rearrange("p (j h d) -> p j h d", h=HEADS, d=HD),
                                                  w, ALU.mult)
                ins.then_inc(low_used, 1)

            def weigh(b, j, beside):
                if j == 0:
                    dve.wait_ge(v_shifted, upto(b, N_SHIFT_DMA, N_SHIFT_DMA))
                if j >= TERM_BUFS:
                    dve.wait_ge(terms_summed, upto(b, NT, j - TERM_BUFS + 1))
                n = 1 + min(j // 2, 2)

                def term(m0, m1, src):
                    w = wgt[:, j, m0:m1, :].unsqueeze(3).to_broadcast([P, m1 - m0, HEADS, HD])
                    dst = terms[:, j % TERM_BUFS, m0:m1, :].rearrange("p m (h d) -> p m h d", d=HD)
                    return nc.vector.tensor_tensor(dst, src.rearrange("p m (h d) -> p m h d", d=HD), w, ALU.mult)

                if n > 1:
                    term(M_TILES + 3 - n, M_TILES + 3, v_tok[:, j - 2 * (n - 1):j + 1:2, :])
                else:
                    term(M_TILES + 2, M_TILES + 3, v_tok[:, j:j + 1, :])
                beside(0)
                if j >= 1:
                    term(M_128, M_128 + 1, v_tok[:, j - 1:j, :])
                beside(1)
                term(M_SHIFT, M_LOW, v_shift[:, :, j, :]).then_inc(terms_ready, 1)
                beside(2)

            def add_conv(b, half):
                dve.wait_ge(terms_summed, upto(b, NT, TPH * (half + 1)))
                dve.wait_ge(conv_step, upto(b, N_CONV_STEPS, N_CONV_STEPS))
                cols = bass.ts(half, HALF)
                nc.vector.tensor_tensor(hT[:, cols], psH[:], convT[:, cols], ALU.add).then_inc(hT_ready, 1)

            def add_normed(b, half):
                dve.wait_ge(y_ready, upto(b, 2, half + 1))
                dve.wait_ge(xn_kept, upto(b, 1, 1))
                tiles = slice(half * TPH, (half + 1) * TPH)
                nc.vector.tensor_tensor(yc[:, tiles, :], psY[:].rearrange("p (j c) -> p j c", c=P),
                                        xn_res[:, tiles, :], ALU.add).then_inc(yc_ready, 1)

            def residual(u, beside=lambda n: None):
                b, half = u // 2, u % 2
                dve.wait_ge(x_res_ld, upto(b, N_DMA, 16))
                dve.wait_ge(ln2_ready, u + 1)
                if 0 < b < B - 1:
                    dve.wait_ge(out_ready[half], upto(b, TPH, 0))
                for j in range(half * TPH, (half + 1) * TPH):
                    nc.vector.scalar_tensor_tensor(out=x2_of(u)[:, j, :], in0=yc[:, j, :], scalar=rstd2[:, j:j + 1],
                                                   in1=x_res[:, j, :], op0=ALU.mult, op1=ALU.add).then_inc(x2_ready, 1)
                    beside(j % TPH)

            def gates(u, steps):
                bc = [P, TPH, EXPERTS]
                den_, sig, score, eq, cand, one1, rest, one2, both, g = (t[:] for t in gtmp)
                m1, c1, m2, c2, msum, mrec = (t[:] for t in gmax)
                tt, ts, red = nc.vector.tensor_tensor, nc.vector.tensor_scalar, nc.vector.tensor_reduce
                rec, copy = nc.vector.reciprocal, nc.vector.tensor_copy

                def spread(t):
                    return t.unsqueeze(2).to_broadcast(bc)

                for n in steps:
                    if n == 0:
                        dve.wait_ge(front_free, upto(u, N_FRONT, 3))
                    if n or u:
                        dve.wait_ge(gate_step, upto(u, N_GATE_STEPS, n))
                    if n == 0:
                        ins = ts(den_, gexp[:], 1.0, None, ALU.add)
                    elif n == 1:
                        ins = rec(sig, den_)
                    elif n == 2:
                        ins = ts(score, sig, rscale[:], None, ALU.mult)
                    elif n == 3:
                        ins = red(m1, score, AX_X, ALU.max)
                    elif n == 4:
                        ins = tt(eq, score, spread(m1), ALU.is_equal)
                    elif n == 5:
                        ins = tt(cand, eq, first_pref[:], ALU.mult)
                    elif n == 6:
                        ins = red(c1, cand, AX_X, ALU.max)
                    elif n == 7:
                        ins = tt(one1, cand, spread(c1), ALU.is_equal)
                    elif n == 8:
                        ins = nc.vector.scalar_tensor_tensor(out=rest, in0=one1, scalar=-BIG, in1=score,
                                                             op0=ALU.mult, op1=ALU.add)
                    elif n == 9:
                        ins = red(m2, rest, AX_X, ALU.max)
                    elif n == 10:
                        ins = tt(eq, rest, spread(m2), ALU.is_equal)
                    elif n == 11:
                        ins = tt(cand, eq, first_pref[:], ALU.mult)
                    elif n == 12:
                        ins = red(c2, cand, AX_X, ALU.max)
                    elif n == 13:
                        ins = tt(one2, cand, spread(c2), ALU.is_equal)
                    elif n == 14:
                        ins = tt(both, one1, one2, ALU.add)
                    elif n == 15:
                        ins = tt(both, both, score, ALU.mult)
                    elif n == 16:
                        ins = tt(msum, m1, m2, ALU.add)
                    elif n == 17:
                        ins = rec(mrec, msum)
                    elif n == 18:
                        ins = tt(g, both, spread(mrec), ALU.mult)
                    elif n == 19:
                        if u:
                            dve.wait_ge(gates_turned, u)
                        ins = copy(gparts[:, :, 0, :], g)
                    elif n == 20:
                        ins = tt(rest, g, gparts[:, :, 0, :], ALU.subtract)
                    elif n == 21:
                        ins = copy(gparts[:, :, 1, :], rest)
                    elif n == 22:
                        ins = tt(cand, rest, gparts[:, :, 1, :], ALU.subtract)
                    else:
                        ins = copy(gparts[:, :, 2, :], cand)
                    ins.then_inc(gate_step, 1)

            def gate_hidden(u, chunks):
                cols = bass.ts(u % 2, HALF)
                for c in chunks:
                    dve.wait_ge(gate_spread, upto(u, 4, c + 1))
                    if u >= 2 * B - 2:
                        dve.wait_ge(hidden_free, upto(u, N_HIDDEN, c + 1))
                    nc.vector.tensor_tensor(hid[:, c, cols], hid[:, c, cols], psG[:, c % 2, :],
                                            ALU.mult).then_inc(gated, 1)

            def finish(u):
                if u >= 2:
                    dve.wait_ge(out_stored[u % 2], upto(u // 2, N_DMA, 0))
                for i, part in enumerate(end_parts(u)):
                    dve.wait_ge(ln4_ready, u + 1 + i)
                    for n in part:
                        j = u % 2 * TPH + n
                        nc.vector.scalar_tensor_tensor(out=y_out[:, j, :], in0=output_tile(u, n), scalar=rstd4[:, j:j + 1],
                                                       in1=x2_of(u)[:, j, :], op0=ALU.mult,
                                                       op1=ALU.add).then_inc(out_ready[u % 2], 1)

            stats(0)
            dve.wait_ge(consts_ready, 1)
            dve.wait_ge(zeros_set, 1)
            for b in range(B + 1):
                attn, ffn, more = b < B, b >= 1, b < B - 1
                u0, u1 = 2 * b - 2, 2 * b - 1
                if attn:
                    products(b, 0)
                    if b == 0:
                        key_features(0)
                    query_features(b)
                    if more:
                        stats(b + 1)
                if b == 0:
                    centre_weights()
                if attn:
                    products(b, 1)

                def gate_step_of(u, first):
                    def beside(n):
                        if attn and ffn:
                            gates(u, (first + n,))
                    return beside

                if attn and not more:
                    products(b, 2)
                if attn and b >= 2:
                    finish(u0 - 1)
                if ffn:
                    residual(u1)
                if more:
                    products(b, 2, gate_step_of(u0, 0))
                if attn:
                    linear_state(b, gate_step_of(u0, 2 if more else 0))
                    if b == 0:
                        dve.wait_ge(consts_ready, 2)
                    if ffn:
                        gates(u0, range(4 if more else 2, 24))
                    softmax_logits(b)
                    if ffn:
                        gate_hidden(u0, range(0, 4))
                    softmax_weights(b)
                    weigh_low(b)
                    for j in range(NT):
                        def two_gate_steps(n):
                            if ffn and j < TPH:
                                gates(u1, range(2 * (3 * j + n), 2 * (3 * j + n + 1)))

                        weigh(b, j, two_gate_steps)
                        if ffn:
                            if j in (5, 7):
                                gate_hidden(u1, range(j - 5, j - 3))
                        if j == TPH:
                            add_conv(b, 0)
                        if j == TPH + 1:
                            add_normed(b, 0)
                    residual(2 * b)
                    add_conv(b, 1)
                    if more:
                        key_features(b + 1)
                    add_normed(b, 1)
                else:
                    gates(u0, range(0, 24))
                    done = 0
                    for c, step in enumerate(LAST_GATE_STEPS):
                        gates(u1, range(done, step))
                        gate_hidden(u0, (c,))
                        done = step
                    gates(u1, range(done, N_GATE_STEPS))
                    gate_hidden(u1, range(0, 4))
                    finish(u0 - 1)
                    finish(u0)
                    finish(u1)

        @block.tensor
        def _(pe):
            def claim_psA(b, use, half):
                if use == PSA_X:
                    if b >= 0:
                        pe.wait_ge(scores_read, upto(b, 2, half + 1))
                elif use == PSA_V_TOK:
                    pe.wait_ge(psA_free, freed(b - 1, PSA_V, half))
                else:
                    pe.wait_ge(psA_free, freed(b, use - 1, half))

            def turn(b, use, src, later_half=None):
                for j in range(NT):
                    h, cols = bank(j)
                    if j == TPH and later_half:
                        pe.wait_ge(*later_half)
                    if j % TPH == 0:
                        claim_psA(b, use, h)
                    ins = pe.transpose(psA[:, h, cols], src(j), ident[:])
                    if j % TPH == TPH - 1:
                        ins.then_inc(psA_full, 1)

            def project(b, use, part):
                for half in range(2):
                    claim_psA(b, use, half)
                    pe.matmul(psA[:, half, :], wqkv[:, bass.ts(part, P)], xnT[:, bass.ts(half, HALF)],
                              start=True, stop=True).then_inc(psA_full, 1)

            def turn_x(b):
                pe.wait_ge(xn_ready, upto(b, NT, TPH if b == 0 else NT))
                turn(b - 1, PSA_X, lambda j: xn[:, j, :], later_half=(xn_ready, NT) if b == 0 else None)

            def project_k(b):
                project(b - 1, PSA_K, 1)

            def project_q(b):
                project(b - 1, PSA_Q, 0)

            def project_v(b):
                project(b - 1, PSA_V, 2)

            def token_major_v(b):
                turn(b, PSA_V_TOK, lambda j: vT[:, VPRE + j * P:VPRE + (j + 1) * P])

            def token_major_fk(b):
                pe.wait_ge(fk_ready, upto(b, 1, 1))
                turn(b, PSA_FK_TOK, lambda j: fkT[:, bass.ts(j, P)])

            def linear_state(b, first):
                if not first:
                    pe.wait_ge(yc_ready, upto(b, 2, 0))
                pe.wait_ge(psA_free, freed(b, PSA_FK_TOK, 1))
                for j in range(NT):
                    ins = pe.matmul(psY[:, 0:P], fk_tok[:, j, :], v_tok[:, j, :], start=(j == 0), stop=(j == NT - 1))
                ins.then_inc(kv_summed, 1)

            def sum_heads(b, s):
                pe.wait_ge(prod_ready, upto(b, N_PRODUCTS[2], N_PRODUCTS[s]))
                if s:
                    pe.wait_ge(pool_prod_ready, upto(b, len(POOL_PRODUCTS), s + 1))
                if s == 2:
                    pe.wait_ge(fq_ready, upto(b, 1, 1))
                    pe.wait_ge(kv_ready, upto(b, 1, 1))
                for half in range(2):
                    if s == 0:
                        claim_psA(b, PSA_SCORES, half)
                    cols = bass.ts(half, HALF)
                    for q in range(QUADS):
                        off = TERMS[SLOTS * q + s]
                        none = off == 512 and half == 0
                        if none:
                            continue
                        low = off == LOW
                        ins = pe.matmul(psA[32 * q:32 * q + 32, half, :], ksum_sel[:] if low else slot_sel[:, s, :],
                                        fqT[:, cols] if low else prods[:, QUADS * (s % 2) + q, cols],
                                        start=(s == 0), stop=(s == 2))
                    if s == 2:
                        ins.then_inc(psA_full, 1)
                if s < 2:
                    ins.then_inc(group_summed, 1)

            def turn_scores(b):
                turn(b, PSA_SCORES_T, lambda j: scoresT[:, bass.ts(j, P)])

            def low(b):
                pe.wait_ge(kv_ready, b + 1)
                if b:
                    pe.wait_ge(hT_ready, 2 * b)
                for j in range(NT):
                    dst = (psY if j // TPH else psH)[:, bass.ts(j % TPH, P)]
                    ins = pe.matmul(dst, fqT[:, bass.ts(j, P)], kv[:], start=True, stop=True)
                ins.then_inc(low_ready, 1)

            def sum_terms(b, j):
                pe.wait_ge(terms_ready, upto(b, NT, j + 1))
                if j == 0:
                    pe.wait_ge(low_used, b + 1)
                elif j == TPH:
                    pe.wait_ge(hT_ready, upto(b, 2, 1))
                dst = psH[:, bass.ts(j % TPH, P)]
                pe.matmul(dst, low_terms[:, j, :], ident[:], is_transpose=True, start=True, stop=False)
                live = [m for m in range(NV) if TERMS[m] < P or TERMS[m] // P <= j]
                for m in live:
                    ins = pe.matmul(dst, terms[:, j % TERM_BUFS, m, :], ident[:], is_transpose=True,
                                    start=False, stop=(m == live[-1]))
                ins.then_inc(terms_summed, 1)

            def output(b, half):
                pe.wait_ge(hT_ready, upto(b, 2, half + 1))
                if half:
                    pe.wait_ge(yc_ready, upto(b, 2, 1))
                elif b:
                    pe.wait_ge(out_scaled, b)
                for j in range(TPH * half, TPH * (half + 1)):
                    ins = pe.matmul(psY[:, bass.ts(j % TPH, P)], hT[:, bass.ts(j, P)], wo[:], start=True, stop=True)
                ins.then_inc(y_ready, 1)

            def unit_tiles(u):
                return range(u % 2 * TPH, (u % 2 + 1) * TPH)

            def half_cols(u):
                return bass.ts(u % 2, HALF)

            def turn_x3(u):
                if u == 2 * B - 2:
                    pe.wait_ge(hT_ready, 2 * B)
                elif u == 2 * B - 1:
                    pe.wait_ge(front_free, upto(u, N_FRONT, 0))
                elif u:
                    pe.wait_ge(hidden_free, upto(u, N_HIDDEN, -1))
                pe.wait_ge(xn3_ready, u + 1)
                for n, j in enumerate(unit_tiles(u)):
                    ins = pe.transpose(front(u, X3)[:, bass.ts(n, P)], xn3[:, j, :], ident[:])
                ins.then_inc(front_full, 1)

            def gate_logits(u):
                if u == 2 * B - 2:
                    pe.wait_ge(yc_ready, 2 * B)
                elif u < 2 * B - 2 and u:
                    pe.wait_ge(hidden_free, upto(u, N_HIDDEN, 0))
                pe.wait_ge(front_free, upto(u, N_FRONT, 1))
                pe.matmul(front(u, C4), w1[:, 4 * P:5 * P], x3T[:, half_cols(u)], start=True, stop=True).then_inc(front_full, 1)

            def turn_logits(u):
                pe.wait_ge(front_free, upto(u, N_FRONT, 2))
                for n, j in enumerate(unit_tiles(u)):
                    ins = pe.transpose(front(u, LOGITS)[:, bass.ts(n, EXPERTS)], gate_shared[0:EXPERTS, bass.ts(j, P)],
                                       ident[0:EXPERTS, 0:EXPERTS])
                ins.then_inc(front_full, 1)

            def hidden(u, chunks):
                for c in chunks:
                    k = last_chunk(u, c)
                    if k in (2, 3):
                        pe.wait_ge(front_free, upto(u + 1, N_FRONT, 2))
                    elif k > 3:
                        before = max(i for i in range(k) if LAST_BANKS[i] == LAST_BANKS[k])
                        pe.wait_ge(hidden_free, upto(2 * B - 2, N_HIDDEN, before + 1))
                    elif c >= 2 or k >= 0:
                        pe.wait_ge(hidden_free, upto(u, N_HIDDEN, c - 1))
                    else:
                        pe.wait_ge(front_free, upto(u, N_FRONT, c + 2))
                    pe.matmul(hidden_bank(u, c), w1[:, bass.ts(c, P)], x3T[:, half_cols(u)],
                              start=True, stop=True).then_inc(hidden_full, 1)

            def gates_expert_major(u):
                if 0 < u < 2 * B - 1:
                    pe.wait_ge(gated, upto(u, 4, 0))
                pe.wait_ge(gate_step, upto(u, N_GATE_STEPS, N_GATE_STEPS))
                dst = turned_gates(u)
                for n in range(TPH):
                    ins = pe.transpose(dst[:, bass.ts(n, P)], gparts[:, n].rearrange("p a e -> p (a e)"), identb[:])
                ins.then_inc(gates_turned, 1)

            def spread_gates(u, chunks):
                for c in chunks:
                    if c == 0 and u % 2 == 0 and 0 < u < 2 * B - 2:
                        pe.wait_ge(out_ready[1], upto(u // 2, TPH, 0))
                    if c < 2:
                        pe.wait_ge(gT_ready, u + 1)
                    if c >= 2 or u == 2 * B - 1:
                        pe.wait_ge(gated, upto(u, 4, c - 1))
                    pe.matmul(psG[:, c % 2, :], gate_sel[:, c, :], gT[:, u % 2, :], start=True, stop=True).then_inc(gate_spread, 1)

            def experts_out(u, tiles=range(TPH)):
                if u >= 2 * B - 3:
                    pe.wait_ge(scores_read, 2 * B)
                elif u % 2 == 0:
                    pe.wait_ge(low_used, u // 2 + 2)
                pe.wait_ge(hidden_free, upto(u, N_HIDDEN, 4))
                pe.wait_ge(shared_ready, upto(u, 2, 2))
                for n in tiles:
                    j = u % 2 * TPH + n
                    for c in (CH - 1, *range(CH - 1)):
                        if n == tiles[0] and c < CH - 1:
                            pe.wait_ge(gated, upto(u, 4, c + 1))
                        ins = pe.matmul(output_tile(u, n), hid[:, c, bass.ts(j, P)], w2[:, c, :],
                                        start=(c == CH - 1), stop=(c == CH - 2))
                    if n in [part[-1] for part in end_parts(u)]:
                        ins.then_inc(experts_summed, 1)

            def keep_busy(n, bank=psH):
                for k in range(n):
                    pe.transpose(bank[:, bass.ts(k % TPH, P)], ident[:], ident[:])

            pe.wait_ge(ident_ready, 1)
            keep_busy(WARM_UP, psG[:, 0, :])
            pe.wait_ge(wqkv_ld, 16)
            turn_x(0)
            project_k(0)
            project_q(0)
            project_v(0)
            for b in range(B + 1):
                attn, ffn, more = b < B, b >= 1, b < B - 1
                u0, u1 = 2 * b - 2, 2 * b - 1
                if attn:
                    if b == 0:
                        token_major_v(b)
                        token_major_fk(b)
                        pe.wait_ge(consts_ready, 1)
                    sum_heads(b, 0)
                    if ffn:
                        turn_x3(u0)
                        gate_logits(u0)
                    linear_state(b, b == 0)
                    if ffn:
                        turn_logits(u0)
                    sum_heads(b, 1)
                    if ffn:
                        hidden(u0, range(0, 2))
                    keep_busy(FILL_SUM)
                    sum_heads(b, 2)
                    if ffn:
                        hidden(u0, (2,))
                    turn_scores(b)
                    if ffn:
                        hidden(u0, (3,))
                    low(b)
                    if b == 0:
                        pe.wait_ge(w_centred, 1)
                    if ffn:
                        turn_x3(u1)
                        gates_expert_major(u0)
                    if more:
                        turn_x(b + 1)
                    if ffn:
                        spread_gates(u0, range(0, 2))
                        gate_logits(u1)
                        spread_gates(u0, range(2, 4))
                        turn_logits(u1)
                    if more:
                        project_k(b + 1)
                    if ffn:
                        hidden(u1, range(0, 2))
                    if b == 0:
                        project_q(b + 1)
                    if ffn:
                        experts_out(u0)
                    for j in range(NT):
                        if ffn:
                            if j == 2:
                                hidden(u1, range(2, 4))
                            if j == 4:
                                gates_expert_major(u1)
                            if j in (5, 6):
                                spread_gates(u1, range(2 * (j - 5), 2 * (j - 4)))
                        if more:
                            if j == 1 and b:
                                project_q(b + 1)
                            if j == 5:
                                project_v(b + 1)
                        sum_terms(b, j)
                        if j == TPH:
                            output(b, 0)
                    output(b, 1)
                    if more:
                        token_major_v(b + 1)
                        token_major_fk(b + 1)
                    if ffn:
                        experts_out(u1, range(TPH if more else TPH - 1))
                else:
                    spare = psA[:, 0, :]
                    turn_x3(u0)
                    experts_out(u0 - 1, range(TPH - 1, TPH))
                    gate_logits(u0)
                    keep_busy(FILL_FRONT, spare)
                    turn_logits(u0)
                    hidden(u0, range(0, 2))
                    turn_x3(u1)
                    keep_busy(FILL_FRONT, spare)
                    gate_logits(u1)
                    keep_busy(FILL_FRONT, spare)
                    turn_logits(u1)
                    hidden(u0, range(2, 4))
                    gates_expert_major(u0)
                    spread_gates(u0, range(0, 2))
                    hidden(u1, (0,))
                    spread_gates(u0, (2,))
                    hidden(u1, (1,))
                    spread_gates(u0, (3,))
                    hidden(u1, range(2, 4))
                    gates_expert_major(u1)
                    experts_out(u0, (0,))
                    spread_gates(u1, range(0, 2))
                    experts_out(u0, (1,))
                    spread_gates(u1, (2,))
                    experts_out(u0, (2,))
                    spread_gates(u1, (3,))
                    experts_out(u0, (3,))
                    experts_out(u1)


_INS = ['L0_attn_x', 'L0_attn_Wqkv', 'L0_attn_Wo', 'L0_attn_conv_w', 'L0_ffn_gate_W', 'L0_ffn_W1', 'L0_ffn_b1',
        'L0_ffn_W2', 'L0_ffn_b2', 'L0_ffn_Ws1', 'L0_ffn_bs1', 'L0_ffn_Ws2', 'L0_ffn_bs2', 'L0_ffn_route_scale']


def kernel(**inputs):
    import concourse.bacc as bacc
    from concourse.bass_utils import run_bass_kernel_spmd

    nc = bacc.Bacc("TRN2", target_bir_lowering=False, num_devices=1)
    arrays, args = {}, []
    for name in _INS:
        a = np.ascontiguousarray(inputs[name])
        if a.ndim == 0:
            a = a.reshape(1)
        arrays[name] = a
        args.append(nc.dram_tensor(name, a.shape, mybir.dt.from_np(a.dtype), kind="ExternalInput").ap())
    shape = inputs['L0_attn_x'].shape
    args.append(nc.dram_tensor("out", shape, F32, kind="ExternalOutput").ap())
    block_kernel(nc, *args)
    r = run_bass_kernel_spmd(nc, [arrays], core_ids=[0])
    return r.results[0]["out"]
```
